# Optimizing a Trainium2 kernel written in Bass

```python
import numpy as np
import jax
import jax.numpy as jnp

def _softmax(x, axis=-1):
    return jax.nn.softmax(x, axis=axis)

def _gelu(x):
    return jax.nn.gelu(x, approximate=True)

def _silu(x):
    return jax.nn.silu(x)

def _sigmoid(x):
    return jax.nn.sigmoid(x)

def _layernorm(x, axis=-1, eps=1e-05):
    m = jnp.mean(x, axis=axis, keepdims=True)
    v = jnp.var(x, axis=axis, keepdims=True)
    return (x - m) / jnp.sqrt(v + eps)

def _scatter_add(tgt, idx, src, axis=0):
    return tgt.at[idx].add(src)

def _segment_sum(src, seg, n):
    return jax.ops.segment_sum(src, seg, n)
kernel_name = 'mk_macaron_d1_jaxref_r8_4e8ae1'

def setup_inputs(seed: int=0):
    np.random.seed(seed)
    _w = jnp.asarray

    def _L0_attn_setup():
        import jax, jax.numpy as jnp
        import numpy as np
        import math
        B, L, DM = (2, 256, 128)
        DS, DC, E = (16, 4, 2)
        DI = E * DM
        DR = math.ceil(DM / 16)

        def _n(k, shape, s):
            return jax.random.normal(k, shape, jnp.float32) * s

        def _silu(a):
            return a * jax.nn.sigmoid(a)

        def _mamba_fwd(x, in_proj_w, conv_w, conv_b, x_proj_w, dt_proj_w, dt_proj_b, A_log, D, out_proj_w):
            b = x.shape[0]
            di, ds = A_log.shape
            dr = dt_proj_w.shape[1]
            dc = conv_w.shape[-1]
            xz = jnp.einsum('bld,ed->ble', x, in_proj_w)
            xs, z = (xz[..., :di], xz[..., di:])
            xc = jnp.pad(jnp.swapaxes(xs, 1, 2), ((0, 0), (0, 0), (dc - 1, 0)))
            conv = jax.lax.conv_general_dilated(xc, conv_w, (1,), 'VALID', dimension_numbers=('NCH', 'OIH', 'NCH'), feature_group_count=di)
            u = _silu(jnp.swapaxes(conv + conv_b[None, :, None], 1, 2))
            x_dbl = jnp.einsum('bld,ed->ble', u, x_proj_w)
            dt = jax.nn.softplus(jnp.einsum('blr,dr->bld', x_dbl[..., :dr], dt_proj_w) + dt_proj_b)
            Bm = x_dbl[..., dr:dr + ds]
            Cm = x_dbl[..., dr + ds:]
            A = -jnp.exp(A_log)

            def step(h, inp):
                dt_t, B_t, C_t, u_t = inp
                dA = jnp.exp(dt_t[..., None] * A)
                h = h * dA + (dt_t * u_t)[..., None] * B_t[:, None, :]
                y = jnp.einsum('bds,bs->bd', h, C_t)
                return (h, y)
            h0 = jnp.zeros((b, di, ds), x.dtype)
            _, ys = jax.lax.scan(step, h0, (jnp.swapaxes(dt, 0, 1), jnp.swapaxes(Bm, 0, 1), jnp.swapaxes(Cm, 0, 1), jnp.swapaxes(u, 0, 1)))
            y = jnp.swapaxes(ys, 0, 1) + u * D
            y = y * _silu(z)
            return jnp.einsum('bld,ed->ble', y, out_proj_w)
        key = jax.random.key(seed)
        ks = jax.random.split(key, 9)
        x = jax.random.normal(ks[0], (B, L, DM), jnp.float32)
        in_proj_w = _n(ks[1], (2 * DI, DM), DM ** (-0.5))
        conv_w = _n(ks[2], (DI, 1, DC), 0.3)
        conv_b = _n(ks[3], (DI,), 0.02)
        x_proj_w = _n(ks[4], (DR + 2 * DS, DI), DI ** (-0.5))
        dt_proj_w = _n(ks[5], (DI, DR), DR ** (-0.5))
        u = jax.random.uniform(ks[6], (DI,), jnp.float32)
        dt = jnp.exp(u * (math.log(0.1) - math.log(0.001)) + math.log(0.001))
        dt_proj_b = dt + jnp.log(-jnp.expm1(-dt))
        A_log = jnp.log(jnp.broadcast_to(jnp.arange(1, DS + 1, dtype=jnp.float32), (DI, DS)))
        D = jnp.ones((DI,), jnp.float32)
        out_proj_w = _n(ks[7], (DM, DI), DI ** (-0.5))
        return dict(x=x, in_proj_w=in_proj_w, conv_w=conv_w, conv_b=conv_b, x_proj_w=x_proj_w, dt_proj_w=dt_proj_w, dt_proj_b=dt_proj_b, A_log=A_log, D=D, out_proj_w=out_proj_w)
    _L0_attn_in = _L0_attn_setup()

    def _L0_ffn_setup():
        import jax, jax.numpy as jnp
        import numpy as np
        B, S, H = (4, 256, 128)
        F = 512
        E = 8
        JITTER_EPS = 0.01

        def _sparse_mixer_top2(scores, jitter_eps):
            vals, idx = jax.lax.top_k(scores, 2)
            neg_inf = -jnp.inf
            m1 = vals[:, :1]
            factor1 = jnp.maximum(jnp.abs(scores), m1)
            mask1 = (m1 - scores) / factor1 > 2 * jitter_eps
            p1 = jax.nn.softmax(jnp.where(mask1, neg_inf, scores), axis=-1)
            mult1 = jnp.take_along_axis(p1, idx[:, :1], axis=-1)[:, 0]
            m2 = vals[:, 1:2]
            factor2 = jnp.maximum(jnp.abs(scores), m2)
            mask2 = (m2 - scores) / factor2 > 2 * jitter_eps
            top1_onehot = jnp.arange(scores.shape[-1])[None, :] == idx[:, :1]
            s2 = jnp.where(top1_onehot, neg_inf, scores)
            p2 = jax.nn.softmax(jnp.where(mask2, neg_inf, s2), axis=-1)
            mult2 = jnp.take_along_axis(p2, idx[:, 1:2], axis=-1)[:, 0]
            return (mult1, mult2, idx)
        key = jax.random.key(seed)
        k0, k1, k2, k3, k4 = jax.random.split(key, 5)
        hidden_states = jax.random.normal(k0, (B, S, H), dtype=jnp.float32)
        gate_w = jax.random.normal(k1, (E, H), dtype=jnp.float32) * 0.02
        w1 = jax.random.normal(k2, (E, F, H), dtype=jnp.float32) * 0.02
        w2 = jax.random.normal(k3, (E, H, F), dtype=jnp.float32) * 0.02
        w3 = jax.random.normal(k4, (E, F, H), dtype=jnp.float32) * 0.02
        return {'hidden_states': hidden_states, 'gate_w': gate_w, 'w1': w1, 'w2': w2, 'w3': w3}
    _L0_ffn_in = _L0_ffn_setup()
    _d = {'L0_attn_x': _L0_attn_in['x'], 'L0_attn_in_proj_w': _L0_attn_in['in_proj_w'], 'L0_attn_conv_w': _L0_attn_in['conv_w'], 'L0_attn_conv_b': _L0_attn_in['conv_b'], 'L0_attn_x_proj_w': _L0_attn_in['x_proj_w'], 'L0_attn_dt_proj_w': _L0_attn_in['dt_proj_w'], 'L0_attn_dt_proj_b': _L0_attn_in['dt_proj_b'], 'L0_attn_A_log': _L0_attn_in['A_log'], 'L0_attn_D': _L0_attn_in['D'], 'L0_attn_out_proj_w': _L0_attn_in['out_proj_w'], 'L0_ffn_gate_w': _L0_ffn_in['gate_w'], 'L0_ffn_w1': _L0_ffn_in['w1'], 'L0_ffn_w2': _L0_ffn_in['w2'], 'L0_ffn_w3': _L0_ffn_in['w3']}
    _x0 = _d['L0_attn_x']
    _d['L0_attn_x'] = jax.random.normal(jax.random.fold_in(jax.random.key(seed), 1), (4, 512, 128), dtype=_x0.dtype)
    del _x0
    return _d

def reference(L0_attn_x, L0_attn_in_proj_w, L0_attn_conv_w, L0_attn_conv_b, L0_attn_x_proj_w, L0_attn_dt_proj_w, L0_attn_dt_proj_b, L0_attn_A_log, L0_attn_D, L0_attn_out_proj_w, L0_ffn_gate_w, L0_ffn_w1, L0_ffn_w2, L0_ffn_w3):

    def _L0_attn_ref(x, in_proj_w, conv_w, conv_b, x_proj_w, dt_proj_w, dt_proj_b, A_log, D, out_proj_w):
        import jax, jax.numpy as jnp
        import numpy as np
        import math
        B, L, DM = (2, 256, 128)
        DS, DC, E = (16, 4, 2)
        DI = E * DM
        DR = math.ceil(DM / 16)

        def _n(k, shape, s):
            return jax.random.normal(k, shape, jnp.float32) * s

        def _silu(a):
            return a * jax.nn.sigmoid(a)

        def _mamba_fwd(x, in_proj_w, conv_w, conv_b, x_proj_w, dt_proj_w, dt_proj_b, A_log, D, out_proj_w):
            b = x.shape[0]
            di, ds = A_log.shape
            dr = dt_proj_w.shape[1]
            dc = conv_w.shape[-1]
            xz = jnp.einsum('bld,ed->ble', x, in_proj_w)
            xs, z = (xz[..., :di], xz[..., di:])
            xc = jnp.pad(jnp.swapaxes(xs, 1, 2), ((0, 0), (0, 0), (dc - 1, 0)))
            conv = jax.lax.conv_general_dilated(xc, conv_w, (1,), 'VALID', dimension_numbers=('NCH', 'OIH', 'NCH'), feature_group_count=di)
            u = _silu(jnp.swapaxes(conv + conv_b[None, :, None], 1, 2))
            x_dbl = jnp.einsum('bld,ed->ble', u, x_proj_w)
            dt = jax.nn.softplus(jnp.einsum('blr,dr->bld', x_dbl[..., :dr], dt_proj_w) + dt_proj_b)
            Bm = x_dbl[..., dr:dr + ds]
            Cm = x_dbl[..., dr + ds:]
            A = -jnp.exp(A_log)

            def step(h, inp):
                dt_t, B_t, C_t, u_t = inp
                dA = jnp.exp(dt_t[..., None] * A)
                h = h * dA + (dt_t * u_t)[..., None] * B_t[:, None, :]
                y = jnp.einsum('bds,bs->bd', h, C_t)
                return (h, y)
            h0 = jnp.zeros((b, di, ds), x.dtype)
            _, ys = jax.lax.scan(step, h0, (jnp.swapaxes(dt, 0, 1), jnp.swapaxes(Bm, 0, 1), jnp.swapaxes(Cm, 0, 1), jnp.swapaxes(u, 0, 1)))
            y = jnp.swapaxes(ys, 0, 1) + u * D
            y = y * _silu(z)
            return jnp.einsum('bld,ed->ble', y, out_proj_w)
        return _mamba_fwd(x, in_proj_w, conv_w, conv_b, x_proj_w, dt_proj_w, dt_proj_b, A_log, D, out_proj_w)

    def _L0_ffn_ref(hidden_states, gate_w, w1, w2, w3):
        import jax, jax.numpy as jnp
        import numpy as np
        B, S, H = (4, 256, 128)
        F = 512
        E = 8
        JITTER_EPS = 0.01

        def _sparse_mixer_top2(scores, jitter_eps):
            vals, idx = jax.lax.top_k(scores, 2)
            neg_inf = -jnp.inf
            m1 = vals[:, :1]
            factor1 = jnp.maximum(jnp.abs(scores), m1)
            mask1 = (m1 - scores) / factor1 > 2 * jitter_eps
            p1 = jax.nn.softmax(jnp.where(mask1, neg_inf, scores), axis=-1)
            mult1 = jnp.take_along_axis(p1, idx[:, :1], axis=-1)[:, 0]
            m2 = vals[:, 1:2]
            factor2 = jnp.maximum(jnp.abs(scores), m2)
            mask2 = (m2 - scores) / factor2 > 2 * jitter_eps
            top1_onehot = jnp.arange(scores.shape[-1])[None, :] == idx[:, :1]
            s2 = jnp.where(top1_onehot, neg_inf, scores)
            p2 = jax.nn.softmax(jnp.where(mask2, neg_inf, s2), axis=-1)
            mult2 = jnp.take_along_axis(p2, idx[:, 1:2], axis=-1)[:, 0]
            return (mult1, mult2, idx)
        Bv, Sv, Hv = hidden_states.shape
        x = hidden_states.reshape(-1, Hv)
        scores = x @ gate_w.T
        mult1, mult2, idx = _sparse_mixer_top2(scores, JITTER_EPS)
        out = jnp.zeros_like(x)
        for e in range(E):
            w_tok = mult1 * (idx[:, 0] == e) + mult2 * (idx[:, 1] == e)
            h = jax.nn.silu(x @ w1[e].T) * (x @ w3[e].T)
            out = out + w_tok[:, None] * (h @ w2[e].T)
        return out.reshape(Bv, Sv, Hv)
    x = L0_attn_x
    x = x + 0.5 * _L0_ffn_ref(_layernorm(x, axis=-1), L0_ffn_gate_w, L0_ffn_w1, L0_ffn_w2, L0_ffn_w3)
    x = x + _L0_attn_ref(_layernorm(x, axis=-1), L0_attn_in_proj_w, L0_attn_conv_w, L0_attn_conv_b, L0_attn_x_proj_w, L0_attn_dt_proj_w, L0_attn_dt_proj_b, L0_attn_A_log, L0_attn_D, L0_attn_out_proj_w)
    x = x + 0.5 * _L0_ffn_ref(_layernorm(x, axis=-1), L0_ffn_gate_w, L0_ffn_w1, L0_ffn_w2, L0_ffn_w3)
    return x

_drawn_inputs = setup_inputs


def setup_inputs(seed=0):
    import zlib

    import numpy as np

    out = dict(_drawn_inputs(seed))
    spreads = {'L0_attn_D': (1.0, 0.2)}
    factors = {'L0_attn_conv_b': 8.0,
     'L0_attn_x_proj_w': 4.493,
     'L0_attn_dt_proj_w': 8.0,
     'L0_attn_dt_proj_b': 7.653,
     'L0_attn_A_log': 8.0,
     'L0_ffn_gate_w': 4.222,
     'L0_ffn_w1': 3.663,
     'L0_ffn_w2': 3.653,
     'L0_ffn_w3': 3.638}
    for name, (base, spread) in spreads.items():
        noise = np.random.default_rng([zlib.crc32(name.encode()), seed]).standard_normal(out[name].shape)
        drawn = base * np.exp(spread * noise) if base else spread * noise
        out[name] = jnp.asarray(drawn.astype(out[name].dtype))
    for name, factor in factors.items():
        out[name] = (out[name] * factor).astype(out[name].dtype)
    return out
```

```python
from contextlib import ExitStack

import concourse.bass as bass
from concourse import mybir

B, L, H = 4, 512, 128
TILES = L // 128
F, E = 512, 8
FC = F // 128
DI, DS, DC, DR = 256, 16, 4, 8
DH = DI // 128
LN_EPS = 1e-5
JITTER = 2 * 0.01
BC_ROWS = 96
RING_A = 4
STATE_POSITIONS = 2.25
RING_H = 5


def schedule():
    between = {}

    def put(at, *steps):
        between.setdefault(int(at), []).extend(steps)

    for b in range(1, B):
        put(0, ("norm", "in", b), ("turn", "in", b))
    put(1, ("gate", "in", 0))
    for b in range(B):
        put(3 + b, ("gate_turn", "in", b))

    def mixer(b, at, free):
        put(at, ("post", 1, b), ("norm", "mid", b))
        put(at + 2, ("turn", "mid", b))
        at = max(at + 3, free - 3)
        put(at, ("in_proj", b, 0))
        put(at + 1, ("in_proj", b, 1), ("conv", b))
        at = max(at + 2, free + 1)
        put(at, ("in_proj", b, 2))
        put(at + 1, ("in_proj", b, 3))
        put(at + 2, ("x_dbl", b))
        put(at + 3, ("dt_proj", b, 0))
        put(at + 4, ("dt_proj", b, 1), ("softplus", b))
        at += 6
        put(at, ("decays", b, 0))
        put(at + 1, ("drive", b, 0))
        at += 1
        for s in range(DS):
            x = at + s * STATE_POSITIONS
            if s % 2 == 0 and s + 2 < DS:
                put(x + 1, ("decays", b, s // 2 + 1))
            put(x, ("scan", b, s, 0))
            put(x + STATE_POSITIONS / 3, ("scan", b, s, 1))
            if s + 1 < DS:
                put(x + 2 * STATE_POSITIONS / 3, ("drive", b, s + 1))
            put(x + 2 * STATE_POSITIONS / 3, ("read", b, s))
        at = int(at + DS * STATE_POSITIONS) + 1
        put(at, ("out_proj", b), ("norm", "out", b))
        put(at + 2, ("turn", "out", b))
        put(at + 3, ("gate", "out", b))
        put(at + 6, ("gate_turn", "out", b))
        return at, at + 7

    steps, jobs = [("norm", "in", 0), ("turn", "in", 0)], []
    left = {1: [(1, b, e) for b in range(B) for e in range(E)],
            2: [(2, b, e) for b in range(B) for e in range(E)]}
    at, free, ready = 0, 0, {}
    owed = []

    def pay(n):
        for _ in range(min(n, len(owed))):
            steps.append(owed.pop(0))

    while left[1] or left[2]:
        k = len(jobs)
        can = left[2] and ready.get(left[2][0][1], 10 ** 9) <= at
        if can and (not left[1] or jobs[-1][0] == 1):
            job = left[2].pop(0)
        elif left[1]:
            job = left[1].pop(0)
        else:
            pay(FC + 1)
            for p in sorted(p for p in between if p <= at):
                steps += between.pop(p)
            at += 1
            continue
        jobs.append(job)
        for f in range(FC):
            if job[:2] == (1, 0) and f == 0:
                steps.append(("split", job[2]))
            steps.append(("up", k, f))
            pay(2 if f == 0 else 1)
            for p in sorted(p for p in between if p <= at):
                steps += between.pop(p)
            at += 1
        owed += [("spread", k)] + [("down", k, f) for f in range(FC)]
        if job[2] == E - 1:
            if job[0] == 1:
                free, ready[job[1]] = mixer(job[1], at + FC, free)
            else:
                put(at + FC, ("post", 2, job[1]))
    pay(FC + 1)
    for p in sorted(between):
        steps += between[p]
    return steps, jobs


def macaron_kernel(nc: bass.Bass, x, w13, w2, gate, in_proj, vecs, a_log, x_proj, dt_proj, out_proj,
                   ident, pick, rank, out):
    fp32, fp32r, bf16 = mybir.dt.float32, mybir.dt.float32r, mybir.dt.bfloat16
    ALU, ACT, AX = mybir.AluOpType, mybir.ActivationFunctionType, mybir.AxisListType

    STEPS, JOBS = schedule()
    SCRATCH_STAGES = ("turn", "gate", "gate_turn", "spread", "post", "in_proj", "x_dbl", "dt_proj",
                      "out_proj")
    USE, NORM, GATE, HALVED = {}, {}, {}, {}
    for step in STEPS:
        if step[0] in SCRATCH_STAGES:
            USE[step] = len(USE)
        if step[0] == "norm":
            NORM[step] = len(NORM)
        if step[0] == "gate":
            GATE[step] = len(GATE)
        if step[0] == "turn" and step[1] != "mid":
            HALVED[step] = len(HALVED)
    LAST_JOB = {(ffn, b): k for k, (ffn, b, e) in enumerate(JOBS)}
    ADDS = [sum(1 for j in JOBS[:k + 1] if j[2]) for k in range(len(JOBS))]
    POSTS = [s for s in STEPS if s[0] == "post"]

    ctx = ExitStack()
    with ctx:
        def sb(name, shape, dt=fp32):
            return ctx.enter_context(nc.sbuf_tensor(name, shape, dt))

        def bank(name, shape=(128, 512), dt=fp32):
            return ctx.enter_context(nc.psum_tensor(name, list(shape), dt))

        def sem(name):
            return ctx.enter_context(nc.semaphore(name))

        w13_hi = sb("w13_hi", [128, E, 2 * F], fp32r)
        w13_lo = sb("w13_lo", [128, E, 2 * F], fp32r)
        w2_sb = sb("w2_sb", [128, E, FC, H])
        gate_sb = sb("gate_sb", [128, E])
        gate_hi = sb("gate_hi", [128, E], fp32r)
        gate_lo = sb("gate_lo", [128, E], fp32r)
        in_w = sb("in_w", [128, 2 * DI])
        vec = sb("vec", [128, DH, DC + 3])
        a_neg = sb("a_neg", [128, DH, DS])
        x_w = sb("x_w", [128, DH, BC_ROWS + DR])
        dt_w = sb("dt_w", [DR, DI])
        out_w = sb("out_w", [128, DH, H])
        eye = sb("eye", [128, 128])
        eye_bf = sb("eye_bf", [128, 128], bf16)
        pick_sb = sb("pick_sb", [128, 40])
        pick_bf = sb("pick_bf", [128, 40], bf16)
        rank_sb = sb("rank_sb", [128, E])
        mhalf = sb("mhalf", [128, TILES])
        res = sb("res", [128, B * TILES, H])
        stats = sb("stats", [128, TILES, 6])
        mv = sb("mv", [128, TILES, 2])
        rstd = sb("rstd", [128, TILES])
        normed = sb("normed", [128, TILES, H])
        x_hi = sb("x_hi", [128, B, L], fp32r)
        x_lo = sb("x_lo", [128, B, L], fp32r)
        act = sb("act", [128, 2, L])
        h = sb("h", [128, RING_H, L])
        wt = sb("wt", [3 * E, B, L], bf16)
        spread = sb("spread", [128, 2, L])
        scaled = sb("scaled", [128, 2, L])
        ysum = sb("ysum", [128, 2, L])
        GT = B * TILES
        score = sb("score", [128, GT, E])
        top = sb("top", [128, 2, GT])
        first = sb("first", [128, GT])
        hot = sb("hot", [128, 2, GT, E])
        gap = sb("gap", [128, 2, GT, E])
        keep = sb("keep", [128, 2, GT, E])
        expo = gap
        gtmp = sb("gtmp", [128, GT, E])
        total = sb("total", [128, 2, GT])
        wparts = sb("wparts", [128, GT, 3, E], bf16)
        xm = sb("xm", [128, L])
        xs = sb("xs", [128, DH, DC - 1 + L])
        u = sb("u", [128, DH, L])
        silu_z = sb("silu_z", [128, DH, L])
        dt = sb("dt", [128, DH, L])
        dtu = sb("dtu", [128, DH, L])
        y = sb("y", [128, DH, L])
        drive = sb("drive", [128, DH, L])
        state = sb("state", [128, DH, L])
        prod = sb("prod", [128, 2, DH, L])
        decay = sb("decay", [128, RING_A, DH * L])
        bc = sb("bc", [BC_ROWS, L], bf16)
        staged = decay
        dt_x, sp_exp, sp_one, sp_ln = drive, state, prod[:, 0], prod[:, 1]
        sp_diff, sp_den = dt, y
        bc_rest = prod[0:BC_ROWS, 0, 0, :]
        dt_low = prod[0:DR, 0, 1, :]
        bc_mid = prod[:, 1, 0, :].bitcast(bf16)[0:BC_ROWS, 0:L]

        ps_a = [bank(f"ps_a{i}") for i in range(2)]
        ps_b = [bank(f"ps_b{i}") for i in range(2)]
        ps_down = bank("ps_down")
        ps_B = bank("ps_B")
        ps_C = bank("ps_C")
        scratch = bank("scratch")
        scratch_bf = scratch[:, :].bitcast(bf16)

        x_in = [sem(f"x_in{b}") for b in range(B)]
        consts_in = sem("consts_in")
        w13_in = [sem(f"w13_in{i}") for i in range(RING_A)]
        w2_in = [sem(f"w2_in{e}") for e in range(E)]
        out_done = sem("out_done")
        consts_cast = sem("consts_cast")
        a_exp = sem("a_exp")
        a_neg_done = sem("a_neg_done")
        w_hi_done = sem("w_hi_done")
        w_lo_done = sem("w_lo_done")
        norm_stats = sem("norm_stats")
        norm_rstd = sem("norm_rstd")
        norm_done = sem("norm_done")
        scratch_ready = sem("scratch_ready")
        scratch_read = sem("scratch_read")
        x_hi_done = sem("x_hi_done")
        gate_gap = sem("gate_gap")
        gate_exp = sem("gate_exp")
        gate_done = sem("gate_done")
        up_done = sem("up_done")
        act_done = sem("act_done")
        h_done = sem("h_done")
        down_done = sem("down_done")
        scaled_done = sem("scaled_done")
        added = sem("added")
        conv_done = sem("conv_done")
        u_done = sem("u_done")
        dt_low_done = sem("dt_low_done")
        bc_hi_done = sem("bc_hi_done")
        bc_done = sem("bc_done")
        sp_abs_done = sem("sp_abs_done")
        sp_exp_done = sem("sp_exp_done")
        sp_one_done = sem("sp_one_done")
        sp_ln_done = sem("sp_ln_done")
        dt_done = sem("dt_done")
        mamba_set = sem("mamba_set")
        decay_done = sem("decay_done")
        B_done = sem("B_done")
        drive_done = sem("drive_done")
        scan_done = sem("scan_done")
        C_done = sem("C_done")
        prod_done = sem("prod_done")
        y_added = sem("y_added")
        gated = sem("gated")
        dve_chain = sem("dve_chain")
        pool_chain = sem("pool_chain")

        N_CONSTS = 10
        block = ctx.enter_context(nc.Block())

        def rows(name, b):
            return res[:, b * TILES:(b + 1) * TILES, :]

        def tile(ap, j):
            return ap[:, j * 128:(j + 1) * 128]

        @block.sync
        def _(sp):
            xv = x.rearrange("(t p) h -> p t h", p=128)
            ov = out.rearrange("(t p) h -> p t h", p=128)

            def load_w13(e):
                if e >= RING_A:
                    sp.wait_ge(w_lo_done, e - RING_A + 1)
                sp.dma_start(staged[:, e % RING_A, :], w13[:, e, :]).then_inc(w13_in[e % RING_A], 16)

            sp.dma_start(rows(res, 0), xv[:, 0:TILES, :]).then_inc(x_in[0], 16)
            load_w13(0)
            sp.dma_start(eye[:, :], ident).then_inc(consts_in, 16)
            sp.dma_start(gate_sb[:, :], gate).then_inc(consts_in, 16)
            sp.dma_start(pick_sb[:, :], pick).then_inc(consts_in, 16)
            sp.dma_start(rank_sb[:, :], rank).then_inc(consts_in, 16)
            load_w13(1)
            sp.dma_start(w2_sb[:, 0], w2[:, 0]).then_inc(w2_in[0], 16)
            load_w13(2)
            load_w13(3)
            for e in range(1, E):
                sp.dma_start(w2_sb[:, e], w2[:, e]).then_inc(w2_in[e], 16)
                if e + 3 < E:
                    load_w13(e + 3)
            for b in range(B):
                sp.wait_ge(scratch_read, USE["post", 2, b] + 1)
                sp.dma_start(ov[:, b * TILES:(b + 1) * TILES, :], rows(res, b)).then_inc(out_done, 16)
            sp.wait_ge(out_done, 16 * B)

        @block.gpsimd
        def _(pool):
            nc.gpsimd.memset(mhalf[:, :], -0.5).then_inc(pool_chain, 1)
            pool.wait_ge(pool_chain, 1)
            chain = [1]

            def norm(kind, b):
                n = NORM["norm", kind, b]
                pool.wait_ge(norm_stats, n + 1)
                nc.gpsimd.tensor_scalar(rstd[:, :], mv[:, :, 1], LN_EPS, None, ALU.add).then_inc(pool_chain, 1)
                chain[0] += 1
                pool.wait_ge(pool_chain, chain[0])
                nc.gpsimd.tensor_tensor(rstd[:, :], rstd[:, :], mhalf[:, :], ALU.pow).then_inc(norm_rstd, 1)

            def down(k, f):
                ffn, b, e = JOBS[k]
                if f < FC - 1 or e == 0:
                    return
                n = ADDS[k]
                pool.wait_ge(scaled_done, k + 1)
                if n > 1:
                    pool.wait_ge(added, n - 1)
                nc.gpsimd.tensor_tensor(ysum[:, ffn - 1, :], ysum[:, ffn - 1, :], scaled[:, n % 2, :],
                                        ALU.add).then_inc(added, 1)

            def read(b, s):
                n = b * DS + s
                pool.wait_ge(prod_done, n + 1)
                if n:
                    pool.wait_ge(y_added, n)
                nc.gpsimd.tensor_tensor(y[:, :, :], y[:, :, :], prod[:, n % 2], ALU.add).then_inc(y_added, 1)

            stages = {"norm": norm, "down": down, "read": read}
            for stage, *which in STEPS:
                if stage in stages:
                    stages[stage](*which)

        @block.scalar
        def _(sc):
            xv = x.rearrange("(t p) h -> p t h", p=128)
            for b in range(1, B):
                sc.dma_start(rows(res, b), xv[:, b * TILES:(b + 1) * TILES, :]).then_inc(x_in[b], 16)
            for dst, src in ((vec, vecs), (a_neg, a_log), (in_w, in_proj), (x_w, x_proj), (dt_w, dt_proj),
                             (out_w, out_proj)):
                at = (slice(None),) * len(dst.shape)
                sc.dma_start(dst[at], src).then_inc(consts_in, 16)

            def split(e):
                sc.wait_ge(w13_in[e % RING_A], 16 * (e // RING_A + 1))
                nc.scalar.activation(w13_hi[:, e, :], staged[:, e % RING_A, :], ACT.Copy).then_inc(w_hi_done, 1)
                if e == 1:
                    sc.wait_ge(consts_in, 16 * (N_CONSTS))
                    nc.scalar.activation(a_neg[:, :, :], a_neg[:, :, :], ACT.Exp).then_inc(a_exp, 1)

            def turn(kind, b):
                n = USE["turn", kind, b]
                sc.wait_ge(scratch_ready, n + 1)
                if kind == "mid":
                    nc.scalar.activation(xm[:, :], scratch[:, :], ACT.Copy).then_inc(scratch_read, 1)
                else:
                    nc.scalar.activation(x_hi[:, b, :], scratch[:, :], ACT.Copy).then_inc(x_hi_done, 1)

            def gate(kind, b):
                n = GATE["gate", kind, b]
                t = GT if kind == "in" else TILES
                sc.wait_ge(gate_gap, n + 1)
                nc.scalar.activation(expo[:, :, 0:t, :], gap[:, :, 0:t, :], ACT.Exp, scale=-1.0).then_inc(gate_exp, 1)

            def gate_turn(kind, b):
                sc.wait_ge(scratch_ready, USE["gate_turn", kind, b] + 1)
                nc.scalar.activation(wt[:, b, :], scratch_bf[0:3 * E, 0:L], ACT.Copy).then_inc(scratch_read, 1)

            def up(k, f):
                g = k * FC + f
                sc.wait_ge(up_done, g + 1)
                if g >= 2:
                    sc.wait_ge(h_done, g - 1)
                nc.scalar.activation(act[:, g % 2, :], ps_a[g % 2][:, :], ACT.Silu).then_inc(act_done, 1)

            def spread_(k):
                sc.wait_ge(scratch_ready, USE["spread", k] + 1)
                if k >= 2:
                    sc.wait_ge(scaled_done, k - 1)
                nc.scalar.activation(spread[:, k % 2, :], scratch[:, :], ACT.Copy).then_inc(scratch_read, 1)

            def in_proj_(b, i):
                sc.wait_ge(scratch_ready, USE["in_proj", b, i] + 1)
                if i < DH:
                    if b:
                        sc.wait_ge(conv_done, DH * b)
                    nc.scalar.activation(xs[:, i, DC - 1:], scratch[:, :], ACT.Copy).then_inc(scratch_read, 1)
                else:
                    if b:
                        sc.wait_ge(gated, b)
                    nc.scalar.activation(silu_z[:, i - DH, :], scratch[:, :], ACT.Silu).then_inc(scratch_read, 1)

            def conv_(b):
                for i in range(DH):
                    sc.wait_ge(conv_done, DH * b + i + 1)
                    nc.scalar.activation(u[:, i, :], u[:, i, :], ACT.Silu,
                                         bias=vec[:, i, DC:DC + 1]).then_inc(u_done, 1)

            def x_dbl(b):
                sc.wait_ge(scratch_ready, USE["x_dbl", b] + 1)
                if b:
                    sc.wait_ge(y_added, DS * b)
                nc.scalar.activation(dt_low[:, :], scratch[BC_ROWS:BC_ROWS + DR, :], ACT.Copy).then_inc(dt_low_done, 1)
                if b:
                    sc.wait_ge(B_done, DS * b)
                    sc.wait_ge(C_done, DS * b)
                nc.scalar.activation(bc[:, :], scratch[0:BC_ROWS, :], ACT.Copy).then_inc(bc_hi_done, 1)

            def softplus(b):
                sc.wait_ge(sp_abs_done, b + 1)
                nc.scalar.activation(sp_exp[:, :, :], sp_exp[:, :, :], ACT.Exp).then_inc(sp_exp_done, 1)
                sc.wait_ge(sp_one_done, b + 1)
                nc.scalar.activation(sp_ln, sp_one, ACT.Ln).then_inc(sp_ln_done, 1)

            def decays(b, w):
                sc.wait_ge(dt_done, b + 1)
                if b == 0 and w == 0:
                    sc.wait_ge(w_lo_done, E)
                    sc.wait_ge(a_neg_done, 1)
                for s in (2 * w, 2 * w + 1):
                    n = b * DS + s
                    if n >= RING_A:
                        sc.wait_ge(scan_done, DH * (n - RING_A + 1))
                    for i in range(DH):
                        nc.scalar.activation(decay[:, n % RING_A, i * L:(i + 1) * L], dt[:, i, :], ACT.Exp,
                                             scale=a_neg[:, i, s:s + 1]).then_inc(decay_done, 1)

            stages = {"split": split, "turn": turn, "gate": gate, "gate_turn": gate_turn, "up": up,
                      "spread": spread_, "in_proj": in_proj_, "conv": conv_, "x_dbl": x_dbl,
                      "softplus": softplus, "decays": decays}
            for stage, *which in STEPS:
                if stage in stages:
                    stages[stage](*which)

        @block.tensor
        def _(pe):
            pe.wait_ge(consts_cast, 1)

            def begin(*step):
                n = USE[step]
                if n:
                    pe.wait_ge(scratch_read, n)
                return n

            def turn(kind, b):
                begin("turn", kind, b)
                pe.wait_ge(norm_done, NORM["norm", kind, b] + 1)
                rows_ = xm[:, :].rearrange("p (t h) -> p t h", h=H) if kind == "mid" else normed
                for j in range(TILES):
                    last = nc.tensor.transpose(tile(scratch, j), rows_[:, j, :], eye[:, :])
                last.then_inc(scratch_ready, 1)

            def gate_(kind, b):
                begin("gate", kind, b)
                batches = range(B) if kind == "in" else (b,)
                for m, bb in enumerate(batches):
                    for j in range(TILES):
                        c = (m * TILES + j) * E
                        for n, (xx, gg) in enumerate(((x_hi, gate_hi), (x_hi, gate_lo), (x_lo, gate_hi))):
                            last = nc.tensor.matmul(scratch[:, c:c + E], tile(xx[:, bb, :], j), gg[:, :],
                                                    start=(n == 0), stop=(n == 2))
                last.then_inc(scratch_ready, 1)

            def gate_turn(kind, b):
                begin("gate_turn", kind, b)
                pe.wait_ge(gate_done, (GATE["gate", kind, 0 if kind == "in" else b]) + 1)
                t = b * TILES if kind == "in" else 0
                for j in range(TILES):
                    last = nc.tensor.transpose(tile(scratch_bf[0:3 * E, :], j),
                                               wparts[:, t + j, :, :].rearrange("p c e -> p (c e)"), eye_bf[:, :])
                last.then_inc(scratch_ready, 1)

            def up(k, f):
                ffn, b, e = JOBS[k]
                g = k * FC + f
                if (ffn, b) == (1, 0) and f == 0:
                    pe.wait_ge(w_lo_done, e + 1)
                if e == 0 and f == 0:
                    pe.wait_ge(scratch_read, USE["turn", "in" if ffn == 1 else "out", b] + 1)
                if g >= 2:
                    pe.wait_ge(h_done, g - 1)
                for bank_, at in ((ps_a[g % 2], f * 128), (ps_b[g % 2], F + f * 128)):
                    hi, lo = w13_hi[:, e, at:at + 128], w13_lo[:, e, at:at + 128]
                    nc.tensor.matmul(bank_[:, :], hi, x_hi[:, b, :], start=True, stop=False)
                    nc.tensor.matmul(bank_[:, :], hi, x_lo[:, b, :], start=False, stop=False)
                    last = nc.tensor.matmul(bank_[:, :], lo, x_hi[:, b, :], start=False, stop=True)
                last.then_inc(up_done, 1)

            def spread_(k):
                ffn, b, e = JOBS[k]
                begin("spread", k)
                nc.tensor.matmul(scratch[:, :], pick_bf[0:3 * E, 32 + e:33 + e].broadcast_to([3 * E, 128]),
                                 wt[:, b, :], start=True, stop=True).then_inc(scratch_ready, 1)

            def down(k, f):
                ffn, b, e = JOBS[k]
                g = k * FC + f
                if f == 0:
                    if (ffn, b) == (1, 0):
                        pe.wait_ge(w2_in[e], 16)
                    if k:
                        pe.wait_ge(scaled_done, k)
                pe.wait_ge(h_done, g + 1)
                nc.tensor.matmul(ps_down[:, :], w2_sb[:, e, f, :], h[:, g % RING_H, :],
                                 start=(f == 0), stop=(f == FC - 1)).then_inc(down_done, 1)

            def post(ffn, b):
                begin("post", ffn, b)
                pe.wait_ge(added, ADDS[LAST_JOB[ffn, b]])
                for j in range(TILES):
                    last = nc.tensor.transpose(tile(scratch, j), tile(ysum[:, ffn - 1, :], j), eye[:, :])
                last.then_inc(scratch_ready, 1)

            def in_proj_(b, i):
                begin("in_proj", b, i)
                if b == 0 and i == 0:
                    pe.wait_ge(consts_in, 16 * (N_CONSTS))
                nc.tensor.matmul(scratch[:, :], tile(in_w, i), xm[:, :], start=True, stop=True).then_inc(scratch_ready, 1)

            def x_dbl(b):
                begin("x_dbl", b)
                pe.wait_ge(u_done, DH * (b + 1))
                for i in range(DH):
                    last = nc.tensor.matmul(scratch[0:BC_ROWS + DR, :], x_w[:, i, :], u[:, i, :],
                                            start=(i == 0), stop=(i == DH - 1))
                last.then_inc(scratch_ready, 1)

            def dt_proj_(b, i):
                begin("dt_proj", b, i)
                pe.wait_ge(dt_low_done, b + 1)
                nc.tensor.matmul(scratch[:, :], tile(dt_w, i), dt_low[:, :], start=True, stop=True)\
                    .then_inc(scratch_ready, 1)

            def drive_(b, s):
                n = b * DS + s
                pe.wait_ge(bc_done, b + 1)
                if n:
                    pe.wait_ge(drive_done, n)
                nc.tensor.matmul(ps_B[:, :], pick_bf[0:BC_ROWS, s:s + 1].broadcast_to([BC_ROWS, 128]), bc[:, :],
                                 start=True, stop=True).then_inc(B_done, 1)

            def read(b, s):
                n = b * DS + s
                if n:
                    pe.wait_ge(prod_done, n)
                nc.tensor.matmul(ps_C[:, :], pick_bf[0:BC_ROWS, DS + s:DS + s + 1].broadcast_to([BC_ROWS, 128]),
                                 bc[:, :], start=True, stop=True).then_inc(C_done, 1)

            def out_proj_(b):
                begin("out_proj", b)
                pe.wait_ge(gated, b + 1)
                for j in range(TILES):
                    for i in range(DH):
                        last = nc.tensor.matmul(tile(scratch, j), tile(y[:, i, :], j), out_w[:, i, :],
                                                start=(i == 0), stop=(i == DH - 1))
                last.then_inc(scratch_ready, 1)

            stages = {"turn": turn, "gate": gate_, "gate_turn": gate_turn, "up": up, "spread": spread_,
                      "down": down, "post": post, "in_proj": in_proj_, "x_dbl": x_dbl, "dt_proj": dt_proj_,
                      "drive": drive_, "read": read, "out_proj": out_proj_}
            for stage, *which in STEPS:
                if stage in stages:
                    stages[stage](*which)

        @block.vector
        def _(dve):
            chain = [0]

            def then(instruction):
                chain[0] += 1
                instruction.then_inc(dve_chain, 1)
                dve.wait_ge(dve_chain, chain[0])

            TT, TS, STT = nc.vector.tensor_tensor, nc.vector.tensor_scalar, nc.vector.scalar_tensor_tensor

            nc.vector.memset(xs[:, :, 0:DC - 1], 0.0)
            dve.wait_ge(consts_in, 16 * (N_CONSTS))
            nc.vector.tensor_copy(eye_bf[:, :], eye[:, :])
            nc.vector.tensor_copy(pick_bf[:, :], pick_sb[:, :])
            then(nc.vector.tensor_copy(gate_hi[:, :], gate_sb[:, :]))
            TT(gate_lo[:, :], gate_sb[:, :], gate_hi[:, :].bitcast(fp32), ALU.subtract).then_inc(consts_cast, 1)

            def split(e):
                dve.wait_ge(w_hi_done, e + 1)
                TT(w13_lo[:, e, :], staged[:, e % RING_A, :], w13_hi[:, e, :].bitcast(fp32),
                   ALU.subtract).then_inc(w_lo_done, 1)
                if e == 1:
                    dve.wait_ge(a_exp, 1)
                    TS(a_neg[:, :, :], a_neg[:, :, :], -1.0, None, ALU.mult).then_inc(a_neg_done, 1)

            def norm(kind, b):
                n = NORM["norm", kind, b]
                xx = rows(res, b)
                if kind == "in":
                    dve.wait_ge(x_in[b], 16)
                else:
                    dve.wait_ge(scratch_read, USE[("post", 1, b) if kind == "mid" else ("out_proj", b)] + 1)
                for j in range(TILES):
                    last = nc.vector.bn_stats(stats[:, j, :], xx[:, j, :])
                then(last)
                for j in range(TILES):
                    last = nc.vector.bn_aggr(mv[:, j, :], stats[:, j, :])
                last.then_inc(norm_stats, 1)
                dve.wait_ge(norm_rstd, n + 1)
                if kind == "mid":
                    dst = xm[:, :].rearrange("p (t h) -> p t h", h=H)
                    if b:
                        dve.wait_ge(scratch_ready, USE["in_proj", b - 1, 2 * DH - 1] + 1)
                else:
                    dst = normed
                    others = [s[1:] for s in STEPS if s[0] == "norm" and s[1] != "mid"]
                    at = others.index((kind, b))
                    if at:
                        dve.wait_ge(scratch_ready, USE[("turn",) + tuple(others[at - 1])] + 1)
                for j in range(TILES):
                    last = TS(dst[:, j, :], xx[:, j, :], mv[:, j, 0:1], rstd[:, j:j + 1], ALU.subtract, ALU.mult)
                last.then_inc(norm_done, 1)

            def turn(kind, b):
                if kind == "mid":
                    return
                dve.wait_ge(x_hi_done, HALVED["turn", kind, b] + 1)
                TT(x_lo[:, b, :], scratch[:, :], x_hi[:, b, :].bitcast(fp32), ALU.subtract).then_inc(scratch_read, 1)

            def gate_(kind, b):
                n = GATE["gate", kind, b]
                use = USE["gate", kind, b]
                t = GT if kind == "in" else TILES

                def each(ap):
                    return ap.unsqueeze(2).broadcast_to([128, t, E])

                sco, siz, tmp, fst = score[:, 0:t, :], keep[:, 1, 0:t, :], gtmp[:, 0:t, :], first[:, 0:t]
                rnk = rank_sb[:, :].unsqueeze(1).broadcast_to([128, t, E])
                dve.wait_ge(scratch_ready, use + 1)
                nc.vector.tensor_copy(sco.rearrange("p t e -> p (t e)"), scratch[:, 0:t * E]).then_inc(scratch_read, 1)
                dve.wait_ge(scratch_read, use + 1)
                STT(siz, sco, -1.0, sco, ALU.mult, ALU.max)
                for i in range(2):
                    m, ht = top[:, i, 0:t], hot[:, i, 0:t, :]
                    src = sco if i == 0 else tmp
                    then(nc.vector.tensor_reduce(m, src, AX.X, ALU.max))
                    TT(gap[:, i, 0:t, :], each(m), sco, ALU.subtract)
                    then(TT(ht, src, each(m), ALU.is_equal))
                    then(TT(ht, ht, rnk, ALU.mult))
                    then(nc.vector.tensor_reduce(fst, ht, AX.X, ALU.max))
                    then(TT(ht, ht, each(fst), ALU.is_equal))
                    if i == 0:
                        then(STT(tmp, ht, -3.0e38, sco, ALU.mult, ALU.add))
                TT(keep[:, 0, 0:t, :], siz, each(top[:, 0, 0:t]), ALU.max)
                last = TT(keep[:, 1, 0:t, :], siz, each(top[:, 1, 0:t]), ALU.max)
                then(last)
                for i in range(2):
                    last = STT(keep[:, i, 0:t, :], keep[:, i, 0:t, :], JITTER, gap[:, i, 0:t, :], ALU.mult, ALU.is_ge)
                then(last)
                for i in range(2):
                    last = TS(gap[:, i, 0:t, :], gap[:, i, 0:t, :], 0.0, None, ALU.max)
                last.then_inc(gate_gap, 1)
                then(TT(keep[:, 1, 0:t, :], keep[:, 1, 0:t, :], hot[:, 0, 0:t, :], ALU.subtract))
                dve.wait_ge(gate_exp, n + 1)
                for i in range(2):
                    last = TT(expo[:, i, 0:t, :], expo[:, i, 0:t, :], keep[:, i, 0:t, :], ALU.mult)
                then(last)
                for i in range(2):
                    last = nc.vector.tensor_reduce(total[:, i, 0:t], expo[:, i, 0:t, :], AX.X, ALU.add)
                then(last)
                then(nc.vector.reciprocal(total[:, :, 0:t], total[:, :, 0:t]))
                for i in range(2):
                    last = TT(hot[:, i, 0:t, :], hot[:, i, 0:t, :], each(total[:, i, 0:t]), ALU.mult)
                then(last)
                w = expo[:, 0, 0:t, :]
                if n:
                    former = [s for s in STEPS if s[0] == "gate_turn"]
                    former = former[former.index(("gate_turn", kind, b)) - 1]
                    dve.wait_ge(scratch_ready, USE[former] + 1)
                then(TT(w, hot[:, 0, 0:t, :], hot[:, 1, 0:t, :], ALU.add))
                then(nc.vector.tensor_copy(wparts[:, 0:t, 0, :], w))
                then(TT(tmp, w, wparts[:, 0:t, 0, :], ALU.subtract))
                then(nc.vector.tensor_copy(wparts[:, 0:t, 1, :], tmp))
                TT(wparts[:, 0:t, 2, :], tmp, wparts[:, 0:t, 1, :], ALU.subtract).then_inc(gate_done, 1)

            def up(k, f):
                g = k * FC + f
                dve.wait_ge(act_done, g + 1)
                if g >= RING_H:
                    dve.wait_ge(down_done, g - RING_H + 1)
                TT(h[:, g % RING_H, :], act[:, g % 2, :], ps_b[g % 2][:, :], ALU.mult).then_inc(h_done, 1)

            def down(k, f):
                ffn, b, e = JOBS[k]
                if f < FC - 1:
                    return
                dve.wait_ge(down_done, (k + 1) * FC)
                dve.wait_ge(scratch_read, USE["spread", k] + 1)
                if e == 0:
                    dst = ysum[:, ffn - 1, :]
                    if b:
                        dve.wait_ge(scratch_ready, USE["post", ffn, b - 1] + 1)
                else:
                    n = ADDS[k]
                    dst = scaled[:, n % 2, :]
                    if n > 2:
                        dve.wait_ge(added, n - 2)
                TT(dst, ps_down[:, :], spread[:, k % 2, :], ALU.mult).then_inc(scaled_done, 1)

            def post(ffn, b):
                dve.wait_ge(scratch_ready, USE["post", ffn, b] + 1)
                xx = rows(res, b).rearrange("p t h -> p (t h)")
                STT(xx, scratch[:, :], 0.5, xx, ALU.mult, ALU.add).then_inc(scratch_read, 1)

            def conv_(b):
                if b:
                    dve.wait_ge(mamba_set, b)
                dve.wait_ge(scratch_read, USE["in_proj", b, DH - 1] + 1)
                for c in range(DC):
                    for i in range(DH):
                        src, tap = xs[:, i, c:c + L], vec[:, i, c:c + 1]
                        if c == 0:
                            last = TS(u[:, i, :], src, tap, None, ALU.mult)
                        else:
                            last = STT(u[:, i, :], src, tap, u[:, i, :], ALU.mult, ALU.add)
                        if c == DC - 1:
                            last.then_inc(conv_done, 1)
                    if c < DC - 1:
                        then(last)

            def x_dbl(b):
                dve.wait_ge(bc_hi_done, b + 1)
                use = USE["x_dbl", b]
                if b:
                    dve.wait_ge(y_added, DS * b)
                TT(bc_rest[:, :], scratch[0:BC_ROWS, :], bc[:, :], ALU.subtract).then_inc(scratch_read, 1)
                dve.wait_ge(scratch_read, use + 1)
                then(nc.vector.tensor_copy(bc_mid[:, :], bc_rest[:, :]))
                nc.vector.tensor_copy(bc[32:64, :], bc_mid[32:64, :])
                TT(bc[64:96, :], bc_rest[64:96, :], bc_mid[64:96, :], ALU.subtract).then_inc(bc_done, 1)

            def dt_proj_(b, i):
                dve.wait_ge(scratch_ready, USE["dt_proj", b, i] + 1)
                TS(dt_x[:, i, :], scratch[:, :], vec[:, i, DC + 1:DC + 2], None, ALU.add).then_inc(scratch_read, 1)

            def softplus(b):
                dve.wait_ge(scratch_read, USE["dt_proj", b, DH - 1] + 1)
                if b:
                    dve.wait_ge(y_added, DS * b)
                    dve.wait_ge(decay_done, DH * DS * b)
                STT(sp_exp[:, :, :], dt_x[:, :, :], -1.0, dt_x[:, :, :], ALU.mult, ALU.min).then_inc(sp_abs_done, 1)
                dve.wait_ge(sp_exp_done, b + 1)
                TS(sp_one, sp_exp[:, :, :], 1.0, None, ALU.add).then_inc(sp_one_done, 1)
                dve.wait_ge(sp_one_done, b + 1)
                dve.wait_ge(u_done, DH * (b + 1))
                then(TS(sp_diff[:, :, :], sp_one, 1.0, None, ALU.subtract))
                then(STT(sp_den[:, :, :], sp_diff[:, :, :], 0.0, sp_diff[:, :, :], ALU.is_equal, ALU.add))
                nc.vector.reciprocal(sp_den[:, :, :], sp_den[:, :, :])
                dve.wait_ge(sp_ln_done, b + 1)
                then(STT(sp_ln, sp_diff[:, :, :], 0.0, sp_ln, ALU.is_equal, ALU.add))
                then(TT(sp_ln, sp_ln, sp_exp[:, :, :], ALU.mult))
                then(TT(sp_ln, sp_ln, sp_den[:, :, :], ALU.mult))
                STT(dt[:, :, :], dt_x[:, :, :], 0.0, sp_ln, ALU.max, ALU.add).then_inc(dt_done, 1)
                for i in range(DH):
                    TS(y[:, i, :], u[:, i, :], vec[:, i, DC + 2:DC + 3], None, ALU.mult)
                dve.wait_ge(dt_done, b + 1)
                TT(dtu[:, :, :], dt[:, :, :], u[:, :, :], ALU.mult).then_inc(mamba_set, 1)

            def drive_(b, s):
                n = b * DS + s
                dve.wait_ge(B_done, n + 1)
                if s == 0:
                    dve.wait_ge(mamba_set, b + 1)
                else:
                    dve.wait_ge(scan_done, DH * n)
                TT(drive[:, :, :], dtu[:, :, :], ps_B[:, :].unsqueeze(1).broadcast_to([128, DH, L]),
                   ALU.mult).then_inc(drive_done, 1)

            def scan(b, s, i):
                n = b * DS + s
                dve.wait_ge(decay_done, DH * n + i + 1)
                dve.wait_ge(drive_done, n + 1)
                if n:
                    dve.wait_ge(prod_done, n)
                nc.vector.tensor_tensor_scan(state[:, i, :], decay[:, n % RING_A, i * L:(i + 1) * L], drive[:, i, :],
                                             0.0, ALU.mult, ALU.add).then_inc(scan_done, 1)

            def read(b, s):
                n = b * DS + s
                dve.wait_ge(C_done, n + 1)
                dve.wait_ge(scan_done, DH * (n + 1))
                if n >= 2:
                    dve.wait_ge(y_added, n - 1)
                TT(prod[:, n % 2], state[:, :, :], ps_C[:, :].unsqueeze(1).broadcast_to([128, DH, L]),
                   ALU.mult).then_inc(prod_done, 1)

            def out_proj_(b):
                dve.wait_ge(y_added, DS * (b + 1))
                TT(y[:, :, :], y[:, :, :], silu_z[:, :, :], ALU.mult).then_inc(gated, 1)
                dve.wait_ge(scratch_ready, USE["out_proj", b] + 1)
                xx = rows(res, b).rearrange("p t h -> p (t h)")
                TT(xx, scratch[:, :], xx, ALU.add).then_inc(scratch_read, 1)

            stages = {"split": split, "norm": norm, "turn": turn, "gate": gate_, "up": up, "down": down,
                      "post": post, "conv": conv_, "x_dbl": x_dbl, "dt_proj": dt_proj_, "softplus": softplus,
                      "drive": drive_, "scan": scan, "read": read, "out_proj": out_proj_}
            for stage, *which in STEPS:
                if stage in stages:
                    stages[stage](*which)


def kernel(L0_attn_x, L0_attn_in_proj_w, L0_attn_conv_w, L0_attn_conv_b, L0_attn_x_proj_w, L0_attn_dt_proj_w,
           L0_attn_dt_proj_b, L0_attn_A_log, L0_attn_D, L0_attn_out_proj_w, L0_ffn_gate_w, L0_ffn_w1,
           L0_ffn_w2, L0_ffn_w3):
    import numpy as np
    import concourse.bacc as bacc
    from concourse.bass_utils import run_bass_kernel_spmd

    def halves(a):
        a = np.asarray(a)
        return a.reshape(DH, 128, -1).transpose(1, 0, 2)

    w1, w3, w2 = (np.asarray(a) for a in (L0_ffn_w1, L0_ffn_w3, L0_ffn_w2))
    xp = np.asarray(L0_attn_x_proj_w)
    pick = np.zeros((128, 40), np.float32)
    for r in range(BC_ROWS):
        pick[r, r % 32] = 1
    for r in range(3 * E):
        pick[r, 32 + r % E] = 1
    arrays = {
        "x": np.asarray(L0_attn_x).reshape(B * L, H),
        "w13": np.concatenate([w1.transpose(2, 0, 1), w3.transpose(2, 0, 1)], axis=2),
        "w2": w2.transpose(2, 0, 1).reshape(FC, 128, E, H).transpose(1, 2, 0, 3),
        "gate": np.asarray(L0_ffn_gate_w).T,
        "in_proj": np.asarray(L0_attn_in_proj_w).T,
        "vecs": np.concatenate([halves(np.asarray(L0_attn_conv_w)[:, 0, :]), halves(L0_attn_conv_b),
                                halves(L0_attn_dt_proj_b), halves(L0_attn_D)], axis=2),
        "a_log": halves(L0_attn_A_log),
        "x_proj": halves(np.concatenate([xp[DR:], xp[DR:], xp[DR:], xp[:DR]], axis=0).T),
        "dt_proj": np.asarray(L0_attn_dt_proj_w).T,
        "out_proj": halves(np.asarray(L0_attn_out_proj_w).T),
        "ident": np.eye(128, dtype=np.float32),
        "pick": pick,
        "rank": np.tile(np.arange(E, 0, -1, dtype=np.float32), (128, 1)),
    }
    arrays = {name: np.ascontiguousarray(a) for name, a in arrays.items()}
    nc = bacc.Bacc("TRN2", target_bir_lowering=False, num_devices=1)
    args = [nc.dram_tensor(name, a.shape, mybir.dt.from_np(a.dtype), kind="ExternalInput").ap()
            for name, a in arrays.items()]
    out = nc.dram_tensor("out", (B * L, H), mybir.dt.float32, kind="ExternalOutput").ap()
    macaron_kernel(nc, *args, out)
    r = run_bass_kernel_spmd(nc, [arrays], core_ids=[0])
    return r.results[0]["out"].reshape(B, L, H)
```

```python
from contextlib import ExitStack

import concourse.bass as bass
from concourse import mybir

B, L, H = 4, 512, 128
TILES = L // 128
F, E = 512, 8
FC = F // 128
DI, DS, DC, DR = 256, 16, 4, 8
DH = DI // 128
LN_EPS = 1e-5
JITTER = 2 * 0.01
BC_ROWS = 96
RING_A = 4
STATE_POSITIONS = 2.0
POOL_CHUNKS = (0, 1, 2, 3)
RING_Q = 4
RING_H = 5


def schedule():
    between = {}

    def put(at, *steps):
        between.setdefault(int(at), []).extend(steps)

    def gates(kind, b, at):
        put(at, ("stats", kind, b))
        put(at + 1, ("norm", kind, b))
        put(at + 3, ("turn", kind, b))
        put(at + 4, ("gate", kind, b))
        put(at + 6, ("weigh", kind, b))
        put(at + 8, ("gate_turn", kind, b))

    put(0, ("gate", "in", 0))
    put(2, ("weigh", "in", 0))
    put(4, ("gate_turn", "in", 0))
    for b in range(1, B):
        gates("in", b, 12 * b)

    def mixer(b, at, free):
        put(at, ("post", 1, b), ("stats", "mid", b))
        put(at + 1, ("norm", "mid", b))
        put(at + 3, ("turn", "mid", b))
        at = max(at + 4, free - 1)
        put(at, ("in_proj", b, 0))
        put(at + 1, ("in_proj", b, 1), ("conv", b))
        put(at + 2, ("in_proj", b, 2))
        put(at + 3, ("conv_silu", b), ("in_proj", b, 3))
        put(at + 4, ("x_dbl", b))
        put(at + 5, ("dt_proj", b, 0))
        put(at + 6, ("dt_proj", b, 1))
        put(at + 7, ("sp_one", b))
        put(at + 8, ("softplus", b))
        at += 9
        put(at, ("decays", b, 0))
        put(at, ("drive", b, 0))
        at += 1
        for s in range(DS):
            x = at + s * STATE_POSITIONS
            if s % 2 == 0 and s + 2 < DS:
                put(x + 1, ("decays", b, s // 2 + 1))
            put(x, ("scan", b, s, 0))
            put(x + STATE_POSITIONS / 3, ("scan", b, s, 1))
            if s + 1 < DS:
                put(x + 2 * STATE_POSITIONS / 3, ("drive", b, s + 1))
            put(x + 2 * STATE_POSITIONS / 3, ("read", b, s))
        at = int(at + DS * STATE_POSITIONS) + 1
        put(at, ("out_proj", b))
        gates("out", b, at)
        return at, at + 9

    steps, jobs = [("stats", "in", 0), ("norm", "in", 0), ("split", 0), ("turn", "in", 0)], []
    left = {1: [(1, b, e) for b in range(B) for e in range(E)],
            2: [(2, b, e) for b in range(B) for e in range(E)]}
    at, free, ready = 0, 0, {}
    owed = []

    def pay(n):
        for _ in range(min(n, len(owed))):
            steps.append(owed.pop(0))

    while left[1] or left[2]:
        k = len(jobs)
        can = left[2] and ready.get(left[2][0][1], 10 ** 9) <= at
        if can and (not left[1] or jobs[-1][0] == 1):
            job = left[2].pop(0)
        elif left[1]:
            job = left[1].pop(0)
        else:
            pay(FC + 1)
            for p in sorted(p for p in between if p <= at):
                steps += between.pop(p)
            at += 1
            continue
        jobs.append(job)
        for f in range(FC):
            if job[:2] == (1, 0) and f == 0 and job[2] + 1 < E:
                steps.append(("split", job[2] + 1))
            steps.append(("up", k, f))
            pay(2 if f == 2 else 1)
            for p in sorted(p for p in between if p <= at):
                steps += between.pop(p)
            at += 1
        owed += [("down", k, 0), ("down", k, 1), ("spread", k), ("down", k, 2), ("down", k, 3)]
        if job[2] == E - 1:
            if job[0] == 1:
                free, ready[job[1]] = mixer(job[1], at + FC, free)
            else:
                put(at + FC, ("post", 2, job[1]))
    pay(FC + 1)
    for p in sorted(between):
        steps += between[p]
    return steps, jobs


def macaron_kernel(nc: bass.Bass, x, w13, w2, gate, in_proj, vecs, a_log, x_proj, dt_proj, out_proj,
                   ident, pick, rank, out):
    fp32, fp32r, bf16 = mybir.dt.float32, mybir.dt.float32r, mybir.dt.bfloat16
    ALU, ACT, AX = mybir.AluOpType, mybir.ActivationFunctionType, mybir.AxisListType

    STEPS, JOBS = schedule()
    SCRATCH_STAGES = ("turn", "gate", "gate_turn", "spread", "post", "in_proj", "x_dbl", "dt_proj",
                      "out_proj")
    USE, NORM, GATE, HALVED = {}, {}, {}, {}
    for step in STEPS:
        if step[0] in SCRATCH_STAGES:
            USE[step] = len(USE)
        if step[0] == "stats":
            NORM[("norm",) + step[1:]] = len(NORM)
        if step[0] == "gate":
            GATE[step] = len(GATE)
        if step[0] == "turn" and step[1] != "mid":
            HALVED[step] = len(HALVED)
    LAST_JOB = {(ffn, b): k for k, (ffn, b, e) in enumerate(JOBS)}
    ADDS = [sum(1 for j in JOBS[:k + 1] if j[2]) for k in range(len(JOBS))]
    POSTS = [s for s in STEPS if s[0] == "post"]

    ctx = ExitStack()
    with ctx:
        def sb(name, shape, dt=fp32):
            return ctx.enter_context(nc.sbuf_tensor(name, shape, dt))

        def bank(name, shape=(128, 512), dt=fp32):
            return ctx.enter_context(nc.psum_tensor(name, list(shape), dt))

        def sem(name):
            return ctx.enter_context(nc.semaphore(name))

        w13_hi = sb("w13_hi", [128, E, 2 * F], fp32r)
        w13_lo = sb("w13_lo", [128, E, 2 * F], fp32r)
        w2_sb = sb("w2_sb", [128, E, FC, H])
        gate_sb = sb("gate_sb", [128, E])
        gate_hi = sb("gate_hi", [128, E], fp32r)
        gate_lo = sb("gate_lo", [128, E], fp32r)
        in_w = sb("in_w", [128, 2 * DI])
        vec = sb("vec", [128, DH, DC + 3])
        a_neg = sb("a_neg", [128, DH, DS])
        x_w = sb("x_w", [128, DH, BC_ROWS + DR])
        dt_w = sb("dt_w", [DR, DI])
        out_w = sb("out_w", [128, DH, H])
        eye = sb("eye", [128, 128])
        eye_bf = sb("eye_bf", [128, 128], bf16)
        pick_sb = sb("pick_sb", [128, 40])
        pick_bf = sb("pick_bf", [128, 40], bf16)
        rank_sb = sb("rank_sb", [128, E])
        mhalf = sb("mhalf", [128, TILES])
        res = sb("res", [128, B * TILES, H])
        stats = sb("stats", [128, TILES, 6])
        mv = sb("mv", [128, 2, TILES, 2])
        rstd = sb("rstd", [128, 2, TILES])
        normed = sb("normed", [128, TILES, H])
        x_hi = sb("x_hi", [128, B, L], fp32r)
        x_lo = sb("x_lo", [128, B, L], fp32r)
        act = sb("act", [128, RING_Q, L])
        h = sb("h", [128, RING_H, L])
        wt = sb("wt", [3 * E, B, L], bf16)
        spread = sb("spread", [128, 2, L])
        scaled = sb("scaled", [128, 2, L])
        ysum = sb("ysum", [128, 2, L])
        GT = TILES
        score = sb("score", [128, GT, E])
        top = sb("top", [128, 2, GT])
        first = sb("first", [128, GT])
        hot = sb("hot", [128, 2, GT, E])
        gap = sb("gap", [128, 2, GT, E])
        keep = sb("keep", [128, 2, GT, E])
        expo = gap
        gtmp = sb("gtmp", [128, GT, E])
        total = sb("total", [128, 2, GT])
        wparts = sb("wparts", [128, GT, 3, E], bf16)
        xm = sb("xm", [128, L])
        xs = sb("xs", [128, DH, DC - 1 + L])
        u = sb("u", [128, DH, L])
        silu_z = sb("silu_z", [128, DH, L])
        dt = sb("dt", [128, DH, L])
        dtu = sb("dtu", [128, DH, L])
        y = sb("y", [128, DH, L])
        drive = sb("drive", [128, DH, L])
        state = sb("state", [128, DH, L])
        prod = sb("prod", [128, 2, DH, L])
        decay = sb("decay", [128, RING_A, DH * L])
        bc = sb("bc", [BC_ROWS, L], bf16)
        staged = decay
        dt_relu, sp_exp, sp_one, sp_ln = drive, state, prod[:, 0], prod[:, 1]
        tanh_u = state
        bc_rest = prod[0:BC_ROWS, 0, 0, :]
        dt_low = prod[0:DR, 0, 1, :]
        bc_mid = prod[:, 1, 0, :].bitcast(bf16)[0:BC_ROWS, 0:L]

        ps_a = [bank(f"ps_a{i}") for i in range(2)]
        ps_b = [bank(f"ps_b{i}") for i in range(2)]
        ps_down = bank("ps_down")
        ps_B = bank("ps_B")
        ps_C = bank("ps_C")
        scratch = bank("scratch")
        scratch_bf = scratch[:, :].bitcast(bf16)

        x_in = [sem(f"x_in{b}") for b in range(B)]
        consts_in = sem("consts_in")
        late_in = sem("late_in")
        w13_in = [sem(f"w13_in{i}") for i in range(RING_A)]
        w2_in = [sem(f"w2_in{e}") for e in range(E)]
        out_done = sem("out_done")
        consts_cast = sem("consts_cast")
        a_exp = sem("a_exp")
        a_neg_done = sem("a_neg_done")
        w_hi_done = sem("w_hi_done")
        w_lo_done = sem("w_lo_done")
        norm_stats = sem("norm_stats")
        norm_rstd = sem("norm_rstd")
        norm_done = sem("norm_done")
        scratch_ready = sem("scratch_ready")
        scratch_read = sem("scratch_read")
        x_hi_done = sem("x_hi_done")
        gate_gap = sem("gate_gap")
        gate_exp = sem("gate_exp")
        gate_done = sem("gate_done")
        up_done = sem("up_done")
        act_done = sem("act_done")
        b_copied = sem("b_copied")
        q_done = sem("q_done")
        h_dve_done = sem("h_dve_done")
        h_pool_done = sem("h_pool_done")
        down_done = sem("down_done")
        scaled_done = sem("scaled_done")
        added = sem("added")
        conv_done = sem("conv_done")
        tanh_u_done = sem("tanh_u_done")
        u_done = sem("u_done")
        tanh_z = sem("tanh_z")
        dt_low_done = sem("dt_low_done")
        bc_hi_done = sem("bc_hi_done")
        bc_done = sem("bc_done")
        sp_exp_done = sem("sp_exp_done")
        sp_one_done = sem("sp_one_done")
        sp_ln_done = sem("sp_ln_done")
        dt_done = sem("dt_done")
        mamba_set = sem("mamba_set")
        decay_done = sem("decay_done")
        B_done = sem("B_done")
        drive_done = sem("drive_done")
        scan_done = sem("scan_done")
        C_done = sem("C_done")
        prod_done = sem("prod_done")
        y_added = sem("y_added")
        gated = sem("gated")
        dve_chain = sem("dve_chain")
        pool_chain = sem("pool_chain")

        EARLY, LATE = 4, 6
        block = ctx.enter_context(nc.Block())

        def rows(name, b):
            return res[:, b * TILES:(b + 1) * TILES, :]

        def tile(ap, j):
            return ap[:, j * 128:(j + 1) * 128]

        def pool_chunks(n):
            return sum(1 for g in range(n % FC) if g in POOL_CHUNKS) + n // FC * len(POOL_CHUNKS)

        def h_is_done(engine, g):
            if g % FC in POOL_CHUNKS:
                engine.wait_ge(h_pool_done, pool_chunks(g + 1))
            else:
                engine.wait_ge(h_dve_done, g + 1 - pool_chunks(g + 1))

        @block.sync
        def _(sp):
            xv = x.rearrange("(t p) h -> p t h", p=128)
            ov = out.rearrange("(t p) h -> p t h", p=128)

            def load_w13(e):
                if e >= RING_A:
                    sp.wait_ge(w_lo_done, e - RING_A + 1)
                sp.dma_start(staged[:, e % RING_A, :], w13[:, e, :]).then_inc(w13_in[e % RING_A], 16)

            sp.dma_start(rows(res, 0), xv[:, 0:TILES, :]).then_inc(x_in[0], 16)
            sp.dma_start(eye[:, :], ident).then_inc(consts_in, 16)
            sp.dma_start(gate_sb[:, :], gate).then_inc(consts_in, 16)
            sp.dma_start(pick_sb[:, :], pick).then_inc(consts_in, 16)
            sp.dma_start(rank_sb[:, :], rank).then_inc(consts_in, 16)
            load_w13(0)
            load_w13(1)
            sp.dma_start(w2_sb[:, 0], w2[:, 0]).then_inc(w2_in[0], 16)
            load_w13(2)
            load_w13(3)
            for e in range(1, E):
                sp.dma_start(w2_sb[:, e], w2[:, e]).then_inc(w2_in[e], 16)
                if e + 3 < E:
                    load_w13(e + 3)
            for b in range(B):
                sp.wait_ge(scratch_read, USE["post", 2, b] + 1)
                sp.dma_start(ov[:, b * TILES:(b + 1) * TILES, :], rows(res, b)).then_inc(out_done, 16)
            sp.wait_ge(out_done, 16 * B)

        @block.gpsimd
        def _(pool):
            nc.gpsimd.memset(mhalf[:, :], -0.5).then_inc(pool_chain, 1)
            pool.wait_ge(pool_chain, 1)
            chain = [1]

            def stats_(kind, b):
                n = NORM["norm", kind, b]
                pool.wait_ge(norm_stats, n + 1)
                nc.gpsimd.tensor_scalar(rstd[:, n % 2, :], mv[:, n % 2, :, 1], LN_EPS, None, ALU.add).then_inc(pool_chain, 1)
                chain[0] += 1
                pool.wait_ge(pool_chain, chain[0])
                nc.gpsimd.tensor_tensor(rstd[:, n % 2, :], rstd[:, n % 2, :], mhalf[:, :], ALU.pow).then_inc(norm_rstd, 1)

            def up(k, f):
                if f not in POOL_CHUNKS:
                    return
                g = k * FC + f
                pool.wait_ge(b_copied, pool_chunks(g + 1))
                pool.wait_ge(q_done, g + 1)
                nc.gpsimd.tensor_tensor(h[:, g % RING_H, :], h[:, g % RING_H, :], act[:, g % RING_Q, :],
                                        ALU.mult).then_inc(h_pool_done, 1)

            def down(k, f):
                ffn, b, e = JOBS[k]
                if f < FC - 1 or e == 0:
                    return
                n = ADDS[k]
                pool.wait_ge(scaled_done, k + 1)
                if n > 1:
                    pool.wait_ge(added, n - 1)
                nc.gpsimd.tensor_tensor(ysum[:, ffn - 1, :], ysum[:, ffn - 1, :], scaled[:, n % 2, :],
                                        ALU.add).then_inc(added, 1)

            def read(b, s):
                n = b * DS + s
                pool.wait_ge(prod_done, n + 1)
                if n:
                    pool.wait_ge(y_added, n)
                nc.gpsimd.tensor_tensor(y[:, :, :], y[:, :, :], prod[:, n % 2], ALU.add).then_inc(y_added, 1)

            stages = {"stats": stats_, "up": up, "down": down, "read": read}
            for stage, *which in STEPS:
                if stage in stages:
                    stages[stage](*which)

        @block.scalar
        def _(sc):
            xv = x.rearrange("(t p) h -> p t h", p=128)
            for b in range(1, B):
                sc.dma_start(rows(res, b), xv[:, b * TILES:(b + 1) * TILES, :]).then_inc(x_in[b], 16)
            for dst, src in ((vec, vecs), (a_neg, a_log), (in_w, in_proj), (x_w, x_proj), (dt_w, dt_proj),
                             (out_w, out_proj)):
                at = (slice(None),) * len(dst.shape)
                sc.dma_start(dst[at], src).then_inc(late_in, 16)

            def split(e):
                sc.wait_ge(w13_in[e % RING_A], 16 * (e // RING_A + 1))
                nc.scalar.activation(w13_hi[:, e, :], staged[:, e % RING_A, :], ACT.Copy).then_inc(w_hi_done, 1)
                if e == 1:
                    sc.wait_ge(late_in, 16 * LATE)
                    nc.scalar.activation(a_neg[:, :, :], a_neg[:, :, :], ACT.Exp).then_inc(a_exp, 1)

            def turn(kind, b):
                n = USE["turn", kind, b]
                sc.wait_ge(scratch_ready, n + 1)
                if kind == "mid":
                    nc.scalar.activation(xm[:, :], scratch[:, :], ACT.Copy).then_inc(scratch_read, 1)
                else:
                    nc.scalar.activation(x_hi[:, b, :], scratch[:, :], ACT.Copy).then_inc(x_hi_done, 1)

            def gate(kind, b):
                n = GATE["gate", kind, b]
                t = TILES
                sc.wait_ge(gate_gap, n + 1)
                nc.scalar.activation(expo[:, :, 0:t, :], gap[:, :, 0:t, :], ACT.Exp, scale=-1.0).then_inc(gate_exp, 1)

            def gate_turn(kind, b):
                sc.wait_ge(scratch_ready, USE["gate_turn", kind, b] + 1)
                nc.scalar.activation(wt[:, b, :], scratch_bf[0:3 * E, 0:L], ACT.Copy).then_inc(scratch_read, 1)

            def up(k, f):
                g = k * FC + f
                sc.wait_ge(up_done, g + 1)
                if g >= RING_Q:
                    h_is_done(sc, g - RING_Q)
                nc.scalar.activation(act[:, g % RING_Q, :], ps_a[g % 2][:, :], ACT.Tanh, scale=0.5).then_inc(act_done, 1)
                if f in POOL_CHUNKS:
                    if g >= RING_H:
                        sc.wait_ge(down_done, g - RING_H + 1)
                    nc.scalar.activation(h[:, g % RING_H, :], ps_b[g % 2][:, :], ACT.Copy).then_inc(b_copied, 1)

            def spread_(k):
                sc.wait_ge(scratch_ready, USE["spread", k] + 1)
                if k >= 2:
                    sc.wait_ge(scaled_done, k - 1)
                nc.scalar.activation(spread[:, k % 2, :], scratch[:, :], ACT.Copy).then_inc(scratch_read, 1)

            def in_proj_(b, i):
                sc.wait_ge(scratch_ready, USE["in_proj", b, i] + 1)
                if i < DH:
                    if b:
                        sc.wait_ge(conv_done, DH * b)
                    nc.scalar.activation(xs[:, i, DC - 1:], scratch[:, :], ACT.Copy).then_inc(scratch_read, 1)
                else:
                    if b:
                        sc.wait_ge(gated, b)
                    nc.scalar.activation(silu_z[:, i - DH, :], scratch[:, :], ACT.Tanh, scale=0.5).then_inc(tanh_z, 1)

            def conv_(b):
                if b:
                    sc.wait_ge(prod_done, DS * b)
                for i in range(DH):
                    sc.wait_ge(conv_done, DH * b + i + 1)
                    nc.scalar.activation(tanh_u[:, i, :], u[:, i, :], ACT.Tanh, scale=0.5).then_inc(tanh_u_done, 1)

            def x_dbl(b):
                sc.wait_ge(scratch_ready, USE["x_dbl", b] + 1)
                if b:
                    sc.wait_ge(y_added, DS * b)
                nc.scalar.activation(dt_low[:, :], scratch[BC_ROWS:BC_ROWS + DR, :], ACT.Copy, scale=0.5).then_inc(dt_low_done, 1)
                if b:
                    sc.wait_ge(B_done, DS * b)
                    sc.wait_ge(C_done, DS * b)
                nc.scalar.activation(bc[:, :], scratch[0:BC_ROWS, :], ACT.Copy, scale=0.5).then_inc(bc_hi_done, 1)

            def dt_proj_(b, i):
                sc.wait_ge(scratch_ready, USE["dt_proj", b, i] + 1)
                bias = vec[:, i, DC + 1:DC + 2]
                nc.scalar.activation(dt_relu[:, i, :], scratch[:, :], ACT.Relu, bias=bias)
                if i:
                    sc.wait_ge(u_done, DH * (b + 1))
                nc.scalar.activation(sp_exp[:, i, :], scratch[:, :], ACT.Abs, bias=bias).then_inc(scratch_read, 1)
                if i == DH - 1:
                    sc.wait_ge(scratch_read, USE["dt_proj", b, i] + 1)
                    nc.scalar.activation(sp_exp[:, :, :], sp_exp[:, :, :], ACT.Exp, scale=-1.0).then_inc(sp_exp_done, 1)

            def sp_one_(b):
                sc.wait_ge(sp_one_done, b + 1)
                nc.scalar.activation(sp_ln, sp_one, ACT.Ln).then_inc(sp_ln_done, 1)

            def decays(b, w):
                sc.wait_ge(dt_done, b + 1)
                if b == 0 and w == 0:
                    sc.wait_ge(w_lo_done, E)
                    sc.wait_ge(a_neg_done, 1)
                for s in (2 * w, 2 * w + 1):
                    n = b * DS + s
                    if n >= RING_A:
                        sc.wait_ge(scan_done, DH * (n - RING_A + 1))
                    for i in range(DH):
                        nc.scalar.activation(decay[:, n % RING_A, i * L:(i + 1) * L], dt[:, i, :], ACT.Exp,
                                             scale=a_neg[:, i, s:s + 1]).then_inc(decay_done, 1)

            stages = {"split": split, "turn": turn, "gate": gate, "gate_turn": gate_turn, "up": up,
                      "spread": spread_, "in_proj": in_proj_, "conv": conv_, "x_dbl": x_dbl,
                      "dt_proj": dt_proj_, "sp_one": sp_one_, "decays": decays}
            for stage, *which in STEPS:
                if stage in stages:
                    stages[stage](*which)

        @block.tensor
        def _(pe):
            pe.wait_ge(consts_cast, 1)

            def begin(*step):
                n = USE[step]
                if n:
                    pe.wait_ge(scratch_read, n)
                return n

            def turn(kind, b):
                begin("turn", kind, b)
                pe.wait_ge(norm_done, NORM["norm", kind, b] + 1)
                rows_ = xm[:, :].rearrange("p (t h) -> p t h", h=H) if kind == "mid" else normed
                for j in range(TILES):
                    last = nc.tensor.transpose(tile(scratch, j), rows_[:, j, :], eye[:, :])
                last.then_inc(scratch_ready, 1)

            def gate_(kind, b):
                begin("gate", kind, b)
                for j in range(TILES):
                    for n, (xx, gg) in enumerate(((x_hi, gate_hi), (x_hi, gate_lo), (x_lo, gate_hi))):
                        last = nc.tensor.matmul(scratch[:, j * E:(j + 1) * E], tile(xx[:, b, :], j), gg[:, :],
                                                start=(n == 0), stop=(n == 2))
                last.then_inc(scratch_ready, 1)

            def gate_turn(kind, b):
                begin("gate_turn", kind, b)
                pe.wait_ge(gate_done, GATE["gate", kind, b] + 1)
                for j in range(TILES):
                    last = nc.tensor.transpose(tile(scratch_bf[0:3 * E, :], j),
                                               wparts[:, j, :, :].rearrange("p c e -> p (c e)"), eye_bf[:, :])
                last.then_inc(scratch_ready, 1)

            def up(k, f):
                ffn, b, e = JOBS[k]
                g = k * FC + f
                if (ffn, b) == (1, 0) and f == 0:
                    pe.wait_ge(w_lo_done, e + 1)
                if e == 0 and f == 0:
                    pe.wait_ge(scratch_read, USE["turn", "in" if ffn == 1 else "out", b] + 1)
                if g >= 2:
                    if f in POOL_CHUNKS:
                        pe.wait_ge(q_done, g - 1)
                        pe.wait_ge(b_copied, pool_chunks(g - 1))
                    else:
                        h_is_done(pe, g - 2)
                for bank_, at in ((ps_a[g % 2], f * 128), (ps_b[g % 2], F + f * 128)):
                    hi, lo = w13_hi[:, e, at:at + 128], w13_lo[:, e, at:at + 128]
                    nc.tensor.matmul(bank_[:, :], hi, x_hi[:, b, :], start=True, stop=False)
                    nc.tensor.matmul(bank_[:, :], hi, x_lo[:, b, :], start=False, stop=False)
                    last = nc.tensor.matmul(bank_[:, :], lo, x_hi[:, b, :], start=False, stop=True)
                last.then_inc(up_done, 1)

            def spread_(k):
                ffn, b, e = JOBS[k]
                begin("spread", k)
                nc.tensor.matmul(scratch[:, :], pick_bf[0:3 * E, 32 + e:33 + e].broadcast_to([3 * E, 128]),
                                 wt[:, b, :], start=True, stop=True).then_inc(scratch_ready, 1)

            def down(k, f):
                ffn, b, e = JOBS[k]
                g = k * FC + f
                if f == 0:
                    if (ffn, b) == (1, 0):
                        pe.wait_ge(w2_in[e], 16)
                    if k:
                        pe.wait_ge(scaled_done, k)
                h_is_done(pe, g)
                nc.tensor.matmul(ps_down[:, :], w2_sb[:, e, f, :], h[:, g % RING_H, :],
                                 start=(f == 0), stop=(f == FC - 1)).then_inc(down_done, 1)

            def post(ffn, b):
                begin("post", ffn, b)
                pe.wait_ge(added, ADDS[LAST_JOB[ffn, b]])
                for j in range(TILES):
                    last = nc.tensor.transpose(tile(scratch, j), tile(ysum[:, ffn - 1, :], j), eye[:, :])
                last.then_inc(scratch_ready, 1)

            def in_proj_(b, i):
                begin("in_proj", b, i)
                if b == 0 and i == 0:
                    pe.wait_ge(late_in, 16 * LATE)
                nc.tensor.matmul(scratch[:, :], tile(in_w, i), xm[:, :], start=True, stop=True).then_inc(scratch_ready, 1)

            def x_dbl(b):
                begin("x_dbl", b)
                pe.wait_ge(u_done, DH * (b + 1))
                for i in range(DH):
                    last = nc.tensor.matmul(scratch[0:BC_ROWS + DR, :], x_w[:, i, :], u[:, i, :],
                                            start=(i == 0), stop=(i == DH - 1))
                last.then_inc(scratch_ready, 1)

            def dt_proj_(b, i):
                begin("dt_proj", b, i)
                pe.wait_ge(dt_low_done, b + 1)
                nc.tensor.matmul(scratch[:, :], tile(dt_w, i), dt_low[:, :], start=True, stop=True)\
                    .then_inc(scratch_ready, 1)

            def drive_(b, s):
                n = b * DS + s
                pe.wait_ge(bc_done, b + 1)
                if n:
                    pe.wait_ge(drive_done, n)
                nc.tensor.matmul(ps_B[:, :], pick_bf[0:BC_ROWS, s:s + 1].broadcast_to([BC_ROWS, 128]), bc[:, :],
                                 start=True, stop=True).then_inc(B_done, 1)

            def read(b, s):
                n = b * DS + s
                if n:
                    pe.wait_ge(prod_done, n)
                nc.tensor.matmul(ps_C[:, :], pick_bf[0:BC_ROWS, DS + s:DS + s + 1].broadcast_to([BC_ROWS, 128]),
                                 bc[:, :], start=True, stop=True).then_inc(C_done, 1)

            def out_proj_(b):
                begin("out_proj", b)
                pe.wait_ge(gated, b + 1)
                for j in range(TILES):
                    for i in range(DH):
                        last = nc.tensor.matmul(tile(scratch, j), tile(y[:, i, :], j), out_w[:, i, :],
                                                start=(i == 0), stop=(i == DH - 1))
                last.then_inc(scratch_ready, 1)

            stages = {"turn": turn, "gate": gate_, "gate_turn": gate_turn, "up": up, "spread": spread_,
                      "down": down, "post": post, "in_proj": in_proj_, "x_dbl": x_dbl, "dt_proj": dt_proj_,
                      "drive": drive_, "read": read, "out_proj": out_proj_}
            for stage, *which in STEPS:
                if stage in stages:
                    stages[stage](*which)

        @block.vector
        def _(dve):
            chain = [0]

            def then(instruction):
                chain[0] += 1
                instruction.then_inc(dve_chain, 1)
                dve.wait_ge(dve_chain, chain[0])

            TT, TS, STT = nc.vector.tensor_tensor, nc.vector.tensor_scalar, nc.vector.scalar_tensor_tensor

            nc.vector.memset(xs[:, :, 0:DC - 1], 0.0)
            dve.wait_ge(consts_in, 16 * EARLY)
            nc.vector.tensor_copy(eye_bf[:, :], eye[:, :])
            nc.vector.tensor_copy(pick_bf[:, :], pick_sb[:, :])
            then(nc.vector.tensor_copy(gate_hi[:, :], gate_sb[:, :]))
            TT(gate_lo[:, :], gate_sb[:, :], gate_hi[:, :].bitcast(fp32), ALU.subtract).then_inc(consts_cast, 1)

            def split(e):
                dve.wait_ge(w_hi_done, e + 1)
                TT(w13_lo[:, e, :], staged[:, e % RING_A, :], w13_hi[:, e, :].bitcast(fp32),
                   ALU.subtract).then_inc(w_lo_done, 1)
                if e == 1:
                    dve.wait_ge(a_exp, 1)
                    TS(a_neg[:, :, :], a_neg[:, :, :], -1.0, None, ALU.mult).then_inc(a_neg_done, 1)

            def stats_(kind, b):
                n = NORM["norm", kind, b]
                xx = rows(res, b)
                if kind == "in":
                    dve.wait_ge(x_in[b], 16)
                else:
                    dve.wait_ge(scratch_read, USE[("post", 1, b) if kind == "mid" else ("out_proj", b)] + 1)
                for j in range(TILES):
                    last = nc.vector.bn_stats(stats[:, j, :], xx[:, j, :])
                then(last)
                for j in range(TILES):
                    last = nc.vector.bn_aggr(mv[:, n % 2, j, :], stats[:, j, :])
                last.then_inc(norm_stats, 1)

            def norm(kind, b):
                n = NORM["norm", kind, b]
                xx = rows(res, b)
                dve.wait_ge(norm_rstd, n + 1)
                if kind == "mid":
                    dst = xm[:, :].rearrange("p (t h) -> p t h", h=H)
                    if b:
                        dve.wait_ge(scratch_ready, USE["in_proj", b - 1, 2 * DH - 1] + 1)
                else:
                    dst = normed
                    others = [s[1:] for s in STEPS if s[0] == "norm" and s[1] != "mid"]
                    at = others.index((kind, b))
                    if at:
                        dve.wait_ge(scratch_ready, USE[("turn",) + tuple(others[at - 1])] + 1)
                for j in range(TILES):
                    last = TS(dst[:, j, :], xx[:, j, :], mv[:, n % 2, j, 0:1], rstd[:, n % 2, j:j + 1], ALU.subtract, ALU.mult)
                last.then_inc(norm_done, 1)

            def turn(kind, b):
                if kind == "mid":
                    return
                dve.wait_ge(x_hi_done, HALVED["turn", kind, b] + 1)
                TT(x_lo[:, b, :], scratch[:, :], x_hi[:, b, :].bitcast(fp32), ALU.subtract).then_inc(scratch_read, 1)

            def gate_(kind, b):
                n = GATE["gate", kind, b]
                use = USE["gate", kind, b]
                t = TILES

                def each(ap):
                    return ap.unsqueeze(2).broadcast_to([128, t, E])

                sco, siz, tmp, fst = score[:, 0:t, :], keep[:, 1, 0:t, :], gtmp[:, 0:t, :], first[:, 0:t]
                rnk = rank_sb[:, :].unsqueeze(1).broadcast_to([128, t, E])
                dve.wait_ge(scratch_ready, use + 1)
                nc.vector.tensor_copy(sco.rearrange("p t e -> p (t e)"), scratch[:, 0:t * E]).then_inc(scratch_read, 1)
                dve.wait_ge(scratch_read, use + 1)
                STT(siz, sco, -1.0, sco, ALU.mult, ALU.max)
                for i in range(2):
                    m, ht = top[:, i, 0:t], hot[:, i, 0:t, :]
                    src = sco if i == 0 else tmp
                    then(nc.vector.tensor_reduce(m, src, AX.X, ALU.max))
                    TT(gap[:, i, 0:t, :], each(m), sco, ALU.subtract)
                    then(TT(ht, src, each(m), ALU.is_equal))
                    then(TT(ht, ht, rnk, ALU.mult))
                    then(nc.vector.tensor_reduce(fst, ht, AX.X, ALU.max))
                    then(TT(ht, ht, each(fst), ALU.is_equal))
                    if i == 0:
                        then(STT(tmp, ht, -3.0e38, sco, ALU.mult, ALU.add))
                TT(keep[:, 0, 0:t, :], siz, each(top[:, 0, 0:t]), ALU.max)
                last = TT(keep[:, 1, 0:t, :], siz, each(top[:, 1, 0:t]), ALU.max)
                then(last)
                for i in range(2):
                    last = STT(keep[:, i, 0:t, :], keep[:, i, 0:t, :], JITTER, gap[:, i, 0:t, :], ALU.mult, ALU.is_ge)
                then(last)
                for i in range(2):
                    last = TS(gap[:, i, 0:t, :], gap[:, i, 0:t, :], 0.0, None, ALU.max)
                last.then_inc(gate_gap, 1)
                then(TT(keep[:, 1, 0:t, :], keep[:, 1, 0:t, :], hot[:, 0, 0:t, :], ALU.subtract))

            def weigh(kind, b):
                n = GATE["gate", kind, b]
                t = TILES

                def each(ap):
                    return ap.unsqueeze(2).broadcast_to([128, t, E])

                tmp = gtmp[:, 0:t, :]
                dve.wait_ge(gate_exp, n + 1)
                for i in range(2):
                    last = TT(expo[:, i, 0:t, :], expo[:, i, 0:t, :], keep[:, i, 0:t, :], ALU.mult)
                then(last)
                for i in range(2):
                    last = nc.vector.tensor_reduce(total[:, i, 0:t], expo[:, i, 0:t, :], AX.X, ALU.add)
                then(last)
                then(nc.vector.reciprocal(total[:, :, 0:t], total[:, :, 0:t]))
                for i in range(2):
                    last = TT(hot[:, i, 0:t, :], hot[:, i, 0:t, :], each(total[:, i, 0:t]), ALU.mult)
                then(last)
                w = expo[:, 0, 0:t, :]
                if n:
                    former = [s for s in STEPS if s[0] == "gate_turn"]
                    former = former[former.index(("gate_turn", kind, b)) - 1]
                    dve.wait_ge(scratch_ready, USE[former] + 1)
                then(TT(w, hot[:, 0, 0:t, :], hot[:, 1, 0:t, :], ALU.add))
                then(nc.vector.tensor_copy(wparts[:, 0:t, 0, :], w))
                then(TT(tmp, w, wparts[:, 0:t, 0, :], ALU.subtract))
                then(nc.vector.tensor_copy(wparts[:, 0:t, 1, :], tmp))
                TT(wparts[:, 0:t, 2, :], tmp, wparts[:, 0:t, 1, :], ALU.subtract).then_inc(gate_done, 1)

            def up(k, f):
                g = k * FC + f
                dve.wait_ge(act_done, g + 1)
                STT(act[:, g % RING_Q, :], act[:, g % RING_Q, :], 1.0, ps_a[g % 2][:, :], ALU.add, ALU.mult).then_inc(q_done, 1)
                if f in POOL_CHUNKS:
                    return
                if g >= RING_H:
                    dve.wait_ge(down_done, g - RING_H + 1)
                dve.wait_ge(q_done, g + 1)
                TT(h[:, g % RING_H, :], act[:, g % RING_Q, :], ps_b[g % 2][:, :], ALU.mult).then_inc(h_dve_done, 1)

            def down(k, f):
                ffn, b, e = JOBS[k]
                if f < FC - 1:
                    return
                dve.wait_ge(down_done, (k + 1) * FC)
                dve.wait_ge(scratch_read, USE["spread", k] + 1)
                if e == 0:
                    dst = ysum[:, ffn - 1, :]
                    if b:
                        dve.wait_ge(scratch_ready, USE["post", ffn, b - 1] + 1)
                else:
                    n = ADDS[k]
                    dst = scaled[:, n % 2, :]
                    if n > 2:
                        dve.wait_ge(added, n - 2)
                TT(dst, ps_down[:, :], spread[:, k % 2, :], ALU.mult).then_inc(scaled_done, 1)

            def post(ffn, b):
                dve.wait_ge(scratch_ready, USE["post", ffn, b] + 1)
                xx = rows(res, b).rearrange("p t h -> p (t h)")
                STT(xx, scratch[:, :], 0.25, xx, ALU.mult, ALU.add).then_inc(scratch_read, 1)

            def conv_(b):
                if b:
                    dve.wait_ge(mamba_set, b)
                dve.wait_ge(scratch_read, USE["in_proj", b, DH - 1] + 1)
                for c in range(DC):
                    for i in range(DH):
                        src, tap = xs[:, i, c:c + L], vec[:, i, c:c + 1]
                        if c == 0:
                            last = TS(u[:, i, :], src, tap, vec[:, i, DC:DC + 1], ALU.mult, ALU.add)
                        else:
                            last = STT(u[:, i, :], src, tap, u[:, i, :], ALU.mult, ALU.add)
                        if c == DC - 1:
                            last.then_inc(conv_done, 1)
                    if c < DC - 1:
                        then(last)

            def conv_silu(b):
                for i in range(DH):
                    dve.wait_ge(tanh_u_done, DH * b + i + 1)
                    STT(u[:, i, :], tanh_u[:, i, :], 1.0, u[:, i, :], ALU.add, ALU.mult).then_inc(u_done, 1)

            def in_proj_(b, i):
                if i >= DH:
                    dve.wait_ge(tanh_z, DH * b + i - DH + 1)
                    STT(silu_z[:, i - DH, :], silu_z[:, i - DH, :], 1.0, scratch[:, :], ALU.add,
                        ALU.mult).then_inc(scratch_read, 1)

            def x_dbl(b):
                dve.wait_ge(bc_hi_done, b + 1)
                use = USE["x_dbl", b]
                if b:
                    dve.wait_ge(y_added, DS * b)
                STT(bc_rest[:, :], scratch[0:BC_ROWS, :], 0.5, bc[:, :], ALU.mult, ALU.subtract).then_inc(scratch_read, 1)
                dve.wait_ge(scratch_read, use + 1)
                then(nc.vector.tensor_copy(bc_mid[:, :], bc_rest[:, :]))
                nc.vector.tensor_copy(bc[32:64, :], bc_mid[32:64, :])
                TT(bc[64:96, :], bc_rest[64:96, :], bc_mid[64:96, :], ALU.subtract).then_inc(bc_done, 1)

            def sp_one_(b):
                dve.wait_ge(sp_exp_done, b + 1)
                TS(sp_one, sp_exp[:, :, :], 1.0, None, ALU.add).then_inc(sp_one_done, 1)

            def softplus(b):
                dve.wait_ge(sp_one_done, b + 1)
                STT(sp_exp[:, :, :], sp_one, -1.0, sp_exp[:, :, :], ALU.add, ALU.subtract)
                dve.wait_ge(sp_ln_done, b + 1)
                then(STT(sp_ln, sp_one, 1.0, sp_ln, ALU.is_gt, ALU.mult))
                then(TT(sp_exp[:, :, :], sp_ln, sp_exp[:, :, :], ALU.subtract))
                if b:
                    dve.wait_ge(decay_done, DH * DS * b)
                TT(dt[:, :, :], dt_relu[:, :, :], sp_exp[:, :, :], ALU.add).then_inc(dt_done, 1)
                for i in range(DH):
                    TS(y[:, i, :], u[:, i, :], vec[:, i, DC + 2:DC + 3], 0.5, ALU.mult, ALU.mult)
                dve.wait_ge(dt_done, b + 1)
                STT(dtu[:, :, :], dt[:, :, :], 0.5, u[:, :, :], ALU.mult, ALU.mult).then_inc(mamba_set, 1)

            def drive_(b, s):
                n = b * DS + s
                dve.wait_ge(B_done, n + 1)
                if s == 0:
                    dve.wait_ge(mamba_set, b + 1)
                else:
                    dve.wait_ge(scan_done, DH * n)
                TT(drive[:, :, :], dtu[:, :, :], ps_B[:, :].unsqueeze(1).broadcast_to([128, DH, L]),
                   ALU.mult).then_inc(drive_done, 1)

            def scan(b, s, i):
                n = b * DS + s
                dve.wait_ge(decay_done, DH * n + i + 1)
                dve.wait_ge(drive_done, n + 1)
                if n:
                    dve.wait_ge(prod_done, n)
                nc.vector.tensor_tensor_scan(state[:, i, :], decay[:, n % RING_A, i * L:(i + 1) * L], drive[:, i, :],
                                             0.0, ALU.mult, ALU.add).then_inc(scan_done, 1)

            def read(b, s):
                n = b * DS + s
                dve.wait_ge(C_done, n + 1)
                dve.wait_ge(scan_done, DH * (n + 1))
                if n >= 2:
                    dve.wait_ge(y_added, n - 1)
                TT(prod[:, n % 2], state[:, :, :], ps_C[:, :].unsqueeze(1).broadcast_to([128, DH, L]),
                   ALU.mult).then_inc(prod_done, 1)

            def out_proj_(b):
                dve.wait_ge(y_added, DS * (b + 1))
                STT(y[:, :, :], y[:, :, :], 0.5, silu_z[:, :, :], ALU.mult, ALU.mult).then_inc(gated, 1)
                dve.wait_ge(scratch_ready, USE["out_proj", b] + 1)
                xx = rows(res, b).rearrange("p t h -> p (t h)")
                TT(xx, scratch[:, :], xx, ALU.add).then_inc(scratch_read, 1)

            stages = {"split": split, "stats": stats_, "norm": norm, "turn": turn, "gate": gate_,
                      "weigh": weigh, "up": up, "down": down,
                      "post": post, "in_proj": in_proj_, "conv": conv_, "conv_silu": conv_silu, "x_dbl": x_dbl,
                      "sp_one": sp_one_, "softplus": softplus, "drive": drive_, "scan": scan, "read": read, "out_proj": out_proj_}
            for stage, *which in STEPS:
                if stage in stages:
                    stages[stage](*which)


def kernel(L0_attn_x, L0_attn_in_proj_w, L0_attn_conv_w, L0_attn_conv_b, L0_attn_x_proj_w, L0_attn_dt_proj_w,
           L0_attn_dt_proj_b, L0_attn_A_log, L0_attn_D, L0_attn_out_proj_w, L0_ffn_gate_w, L0_ffn_w1,
           L0_ffn_w2, L0_ffn_w3):
    import numpy as np
    import concourse.bacc as bacc
    from concourse.bass_utils import run_bass_kernel_spmd

    def halves(a):
        a = np.asarray(a)
        return a.reshape(DH, 128, -1).transpose(1, 0, 2)

    w1, w3, w2 = (np.asarray(a) for a in (L0_ffn_w1, L0_ffn_w3, L0_ffn_w2))
    xp = np.asarray(L0_attn_x_proj_w)
    pick = np.zeros((128, 40), np.float32)
    for r in range(BC_ROWS):
        pick[r, r % 32] = 1
    for r in range(3 * E):
        pick[r, 32 + r % E] = 1
    arrays = {
        "x": np.asarray(L0_attn_x).reshape(B * L, H),
        "w13": np.concatenate([w1.transpose(2, 0, 1), w3.transpose(2, 0, 1)], axis=2),
        "w2": w2.transpose(2, 0, 1).reshape(FC, 128, E, H).transpose(1, 2, 0, 3),
        "gate": np.asarray(L0_ffn_gate_w).T,
        "in_proj": np.asarray(L0_attn_in_proj_w).T,
        "vecs": np.concatenate([halves(np.asarray(L0_attn_conv_w)[:, 0, :]), halves(L0_attn_conv_b),
                                halves(L0_attn_dt_proj_b), halves(L0_attn_D)], axis=2),
        "a_log": halves(L0_attn_A_log),
        "x_proj": halves(np.concatenate([xp[DR:], xp[DR:], xp[DR:], xp[:DR]], axis=0).T),
        "dt_proj": np.asarray(L0_attn_dt_proj_w).T,
        "out_proj": halves(np.asarray(L0_attn_out_proj_w).T),
        "ident": np.eye(128, dtype=np.float32),
        "pick": pick,
        "rank": np.tile(np.arange(E, 0, -1, dtype=np.float32), (128, 1)),
    }
    arrays = {name: np.ascontiguousarray(a) for name, a in arrays.items()}
    nc = bacc.Bacc("TRN2", target_bir_lowering=False, num_devices=1)
    args = [nc.dram_tensor(name, a.shape, mybir.dt.from_np(a.dtype), kind="ExternalInput").ap()
            for name, a in arrays.items()]
    out = nc.dram_tensor("out", (B * L, H), mybir.dt.float32, kind="ExternalOutput").ap()
    macaron_kernel(nc, *args, out)
    r = run_bass_kernel_spmd(nc, [arrays], core_ids=[0])
    return r.results[0]["out"].reshape(B, L, H)
```

```python
from contextlib import ExitStack

import concourse.bass as bass
from concourse import mybir

B, L, H = 4, 512, 128
TILES = L // 128
F, E = 512, 8
FC = F // 128
DI, DS, DC, DR = 256, 16, 4, 8
DH = DI // 128
LN_EPS = 1e-5
JITTER = 2 * 0.01
BC_ROWS = 96
RING_A = 4
GATE_AT = {"stats": 0, "norm": 0.9, "turn": 2.9, "gate": 4.9, "gate_rows": 5.9, "choose": 7.5,
           "gate_exp": 12.5, "weigh": 12.65, "gate_turn": 17.15, "ready": 11.15, "pace": 0.3}
FIRST_GATE_AT = {"gate": 0.075, "gate_rows": 0.3, "choose": 0.5, "gate_exp": 2.138, "weigh": 2.475,
                 "gate_turn": 4, "pace": 0.057}
LAST_GATE_AT = {"stats": 0, "norm": 1, "turn": 1.5, "gate": 2.5, "gate_rows": 3.5, "choose": 3.5,
                "gate_exp": 5.7, "weigh": 5.9, "gate_turn": 7.5, "ready": 2.5, "pace": 0.087}
MID_AT = {"post": 1.1, "stats": 2, "norm": 4, "turn": 6, "in_proj0": 6.25, "in_proj1": 7, "conv": 8,
          "pace": 1.085, "tanh": 0.9, "silu": 1.1, "x_dbl": 2.75, "dt": 3}
FIRST_MID_AT = {"post": 0.5, "stats": 0.5, "norm": 2.5, "turn": 3, "in_proj0": 4, "in_proj1": 5, "conv": 5,
                "pace": 0.4, "tanh": 0.5, "silu": 1, "x_dbl": 0.5, "dt": 2}
DT_AT = {"dt_proj0": 1, "dt_proj1": 2.75, "sp_exp": 3.25, "sp_one": 3.6, "sp_ln": 4, "sp_rest": 4.1,
         "sp_mask": 4.25, "sp_diff": 4.35, "sp_dt": 5.6, "mamba_set": 6, "y_begin": 9.5, "decays": 7.2,
         "B": 7.5, "drive": 8.1, "in_proj2": 10.1, "in_proj3": 11.1, "states": 8.1}
FIRST_DT_AT = {"dt_proj0": 0, "dt_proj1": 0.5, "sp_exp": 2, "sp_one": 2, "sp_ln": 2.25, "sp_rest": 2.6,
               "sp_mask": 2.5, "sp_diff": 3.7, "sp_dt": 4.2, "mamba_set": 4.8, "y_begin": 8.1, "decays": 4.8,
               "B": 5, "drive": 6, "in_proj2": 8.85, "in_proj3": 12.35, "states": 6.1}
STATE_AT = {"decays": 0.625, "scan0": 0, "scan1": 0.32, "B": 1.175, "C": 1.098, "drive": 1.32, "read": 0.892}
PACE = {"0": 2.25, "1": 2.25, "2": 2.2, "3": 2}
END_AT = {"gate_y": 0.1, "out_proj": 2, "norm": 2.9}
LAST_END_AT = {"gate_y": 2, "out_proj": 4, "norm": 4.25}
POST2_AT = 2
IN_AT = 10.5
PAY, SPREAD_AT = (1, 2, 2, 0), 1
CHOOSE_PARTS, WEIGH_PARTS = 13, 9
PARTS = {"choose": CHOOSE_PARTS, "weigh": WEIGH_PARTS}
SCRATCH_STAGES = ("turn", "gate", "gate_rows", "gate_turn", "spread", "post", "in_proj", "x_dbl", "dt_proj", "out_proj")
READ_LATER = ("turn", "gate_rows", "post", "in_proj", "x_dbl", "out_proj")
POOL_CHUNKS = (0, 1, 2, 3)
WARMING = 16
RING_Q = 4
RING_H = 5


def schedule():
    between = {}

    def put(at, *steps):
        between.setdefault(at, []).extend(steps)

    def gates(kind, b, at, where):
        for name in where:
            if name in PARTS:
                for part in range(PARTS[name]):
                    put(at + where[name] + part * where["pace"], (name, kind, b, part))
            elif name not in ("ready", "pace"):
                put(at + where[name], (name, kind, b))

    gates("in", 0, 0, FIRST_GATE_AT)
    for b in range(1, B):
        gates("in", b, IN_AT * b, GATE_AT)

    def mixer(b, at, free):
        mid, dt = (MID_AT, DT_AT) if b else (FIRST_MID_AT, FIRST_DT_AT)
        end, gate_at = (END_AT, GATE_AT) if b < B - 1 else (LAST_END_AT, LAST_GATE_AT)
        put(at + mid["post"], ("post", 1, b))
        for name in ("stats", "norm", "turn"):
            put(at + mid[name], (name, "mid", b))
        for i in range(2):
            put(at + mid[f"in_proj{i}"], ("in_proj", b, i))
        at += mid["conv"]
        pace = mid["pace"]
        for i in range(DH):
            for c in range(DC):
                put(at, ("conv", b, i, c))
                at += pace
            put(at - pace + mid["tanh"], ("tanh_u", b, i))
            put(at - pace + mid["silu"], ("conv_silu", b, i))
        at += mid["silu"] - pace + mid["x_dbl"]
        put(at, ("x_dbl", b))
        at = max(at + mid["dt"] - mid["x_dbl"], free)
        for name in dt:
            if name in ("sp_exp", "sp_one", "sp_ln", "sp_rest", "sp_mask", "sp_diff", "sp_dt", "mamba_set"):
                put(at + dt[name], (name, b))
        put(at + dt["y_begin"], ("y_begin", b))
        for i in range(DH):
            put(at + dt[f"dt_proj{i}"], ("dt_proj", b, i))
            put(at + dt[f"in_proj{DH + i}"], ("in_proj", b, DH + i))
        put(at + dt["decays"], ("decays", b, 0))
        put(at + dt["B"], ("B", b, 0))
        put(at + dt["drive"], ("drive", b, 0))
        at += dt["states"]
        for s in range(DS):
            if s % 2 == 0 and s + 2 < DS:
                put(at + STATE_AT["decays"], ("decays", b, s // 2 + 1))
            for i in range(DH):
                put(at + STATE_AT[f"scan{i}"], ("scan", b, s, i))
            if s + 1 < DS:
                put(at + STATE_AT["B"], ("B", b, s + 1))
                put(at + STATE_AT["drive"], ("drive", b, s + 1))
            put(at + STATE_AT["C"], ("C", b, s))
            put(at + STATE_AT["read"], ("read", b, s))
            at += PACE[str(b)]
        put(at + end["gate_y"], ("gate_y", b))
        put(at + end["out_proj"], ("out_proj", b))
        gates("out", b, at + end["norm"], gate_at)
        return at, at + end["norm"] + gate_at["ready"]

    steps, jobs, late = [], [], []
    left = {1: [(1, b, e) for b in range(B) for e in range(E)],
            2: [(2, b, e) for b in range(B) for e in range(E)]}
    at, free, ready = 0, 0, {}
    owed = []

    def emit(*new):
        for step in new:
            if late and step[0] in SCRATCH_STAGES + ("choose", "stats", "B"):
                steps.append(late.pop())
            steps.append(step)
            if step[0] in READ_LATER and step[:2] != ("turn", "mid"):
                late.append(("read_" + step[0],) + step[1:])

    def emit_between(until):
        for p in sorted(p for p in between if p < until):
            emit(*between.pop(p))
        if late:
            steps.append(late.pop())

    def pay(n):
        for _ in range(min(n, len(owed))):
            emit(owed.pop(0))

    emit(("stats", "in", 0), ("cast",), ("norm", "in", 0), ("split", 0), ("turn", "in", 0))
    emit_between(-1)
    while left[1] or left[2]:
        k = len(jobs)
        can = left[2] and ready.get(left[2][0][1], 10 ** 9) <= at
        if can and (not left[1] or jobs[-1][0] == 1):
            job = left[2].pop(0)
        elif left[1]:
            job = left[1].pop(0)
        else:
            pay(FC + 1)
            emit_between(at + 1)
            at += 1
            continue
        jobs.append(job)
        for f in range(FC):
            if job[:2] == (1, 0) and f == 0 and job[2] + 1 < E:
                emit(("split", job[2] + 1))
            emit(("up", k, f))
            pay(PAY[f])
            emit_between(at + 1)
            at += 1
        owed += [("down", k, f) for f in range(FC)]
        owed.insert(SPREAD_AT, ("spread", k))
        if job[2] == E - 1:
            if job[0] == 1:
                free, ready[job[1]] = mixer(job[1], at + FC, free)
            else:
                put(at + FC + POST2_AT, ("post", 2, job[1]))
    pay(FC + 1)
    emit_between(float("inf"))
    return steps, jobs


def macaron_kernel(nc: bass.Bass, x, w13, w2, gate, in_proj, vecs, a_log, x_proj, dt_proj, out_proj,
                   ident, pick, rank, out):
    fp32, fp32r, bf16 = mybir.dt.float32, mybir.dt.float32r, mybir.dt.bfloat16
    ALU, ACT, AX = mybir.AluOpType, mybir.ActivationFunctionType, mybir.AxisListType

    STEPS, JOBS = schedule()
    assert [s[1:] for s in STEPS if s[0] == "stats"] == [s[1:] for s in STEPS if s[0] == "norm"]
    gating = [s[1:3] for s in STEPS if s[0] in ("choose", "gate_exp", "weigh", "gate_turn")]
    assert all(gating[i] == gating[i - 1] or gating[i] not in gating[:i] for i in range(1, len(gating)))
    USE, NORM, GATE, HALVED = {}, {}, {}, {}
    for step in STEPS:
        if step[0] in SCRATCH_STAGES:
            USE[step] = len(USE)
        if step[0] == "stats":
            NORM[("norm",) + step[1:]] = len(NORM)
        if step[0] == "gate":
            GATE[step] = len(GATE)
        if step[0] == "turn" and step[1] != "mid":
            HALVED[step] = len(HALVED)
    LAST_JOB = {(ffn, b): k for k, (ffn, b, e) in enumerate(JOBS)}
    ADDS = [sum(1 for j in JOBS[:k + 1] if j[2]) for k in range(len(JOBS))]
    POSTS = [s for s in STEPS if s[0] == "post"]

    ctx = ExitStack()
    with ctx:
        def sb(name, shape, dt=fp32):
            return ctx.enter_context(nc.sbuf_tensor(name, shape, dt))

        def bank(name, shape=(128, 512), dt=fp32):
            return ctx.enter_context(nc.psum_tensor(name, list(shape), dt))

        def sem(name):
            return ctx.enter_context(nc.semaphore(name))

        w13_hi = sb("w13_hi", [128, E, 2 * F], fp32r)
        w13_lo = sb("w13_lo", [128, E, 2 * F], fp32r)
        w2_sb = sb("w2_sb", [128, E, FC, H])
        gate_sb = sb("gate_sb", [128, E])
        gate_hi = sb("gate_hi", [128, E], fp32r)
        gate_lo = sb("gate_lo", [128, E], fp32r)
        in_w = sb("in_w", [128, 2 * DI])
        vec = sb("vec", [128, DH, DC + 3])
        a_neg = sb("a_neg", [128, DH, DS])
        x_w = sb("x_w", [128, DH, BC_ROWS + DR])
        dt_w = sb("dt_w", [DR, DI])
        out_w = sb("out_w", [128, DH, H])
        eye = sb("eye", [128, 128])
        eye_bf = sb("eye_bf", [128, 128], bf16)
        pick_sb = sb("pick_sb", [128, 40])
        pick_bf = sb("pick_bf", [128, 40], bf16)
        rank_sb = sb("rank_sb", [128, E])
        mhalf = sb("mhalf", [128, TILES])
        res = sb("res", [128, B * TILES, H])
        stats = sb("stats", [128, TILES, 6])
        mv = sb("mv", [128, 2, TILES, 2])
        rstd = sb("rstd", [128, 2, TILES])
        normed = sb("normed", [128, TILES, H])
        x_hi = sb("x_hi", [128, B, L], fp32r)
        x_lo = sb("x_lo", [128, B, L], fp32r)
        act = sb("act", [128, RING_Q, L])
        h = sb("h", [128, RING_H, L])
        wt = sb("wt", [3 * E, B, L], bf16)
        spread = sb("spread", [128, 2, L])
        scaled = sb("scaled", [128, 2, L])
        ysum = sb("ysum", [128, 2, L])
        score = sb("score", [128, TILES, E])
        top = sb("top", [128, 2, TILES])
        first = sb("first", [128, TILES])
        hot = sb("hot", [128, 2, TILES, E])
        gap = sb("gap", [128, 2, TILES, E])
        keep = sb("keep", [128, 2, TILES, E])
        expo = gap
        gtmp = sb("gtmp", [128, TILES, E])
        total = sb("total", [128, 2, TILES])
        wparts = sb("wparts", [128, TILES, 3, E], bf16)
        xm = sb("xm", [128, L])
        xs = sb("xs", [128, DH, DC - 1 + L])
        u = sb("u", [128, DH, L])
        silu_z = sb("silu_z", [128, DH, L])
        dt = sb("dt", [128, DH, L])
        dtu = sb("dtu", [128, DH, L])
        y = sb("y", [128, DH, L])
        drive = sb("drive", [128, DH, L])
        state = sb("state", [128, DH, L])
        prod = sb("prod", [128, 2, DH, L])
        decay = sb("decay", [128, RING_A, DH * L])
        bc = sb("bc", [BC_ROWS, 2, L], bf16)
        logits = normed[0:E, :, :].rearrange("p t h -> p (t h)")
        staged = decay
        dt_relu, sp_exp, sp_one, sp_ln = drive, state, prod[:, 0], prod[:, 1]
        tanh_u = xs[:, :, DC - 1:]
        bc_rest = xs[0:BC_ROWS, 0, DC - 1:]
        dt_low = xs[0:DR, 1, DC - 1:]

        ps_a = [bank(f"ps_a{i}") for i in range(2)]
        ps_b = [bank(f"ps_b{i}") for i in range(2)]
        ps_down = bank("ps_down")
        ps_B = bank("ps_B")
        ps_C = bank("ps_C")
        scratch = bank("scratch")
        scratch_bf = scratch[:, :].bitcast(bf16)

        x_in = [sem(f"x_in{b}") for b in range(B)]
        consts_in = sem("consts_in")
        late_in = sem("late_in")
        w13_in = [sem(f"w13_in{i}") for i in range(RING_A)]
        w2_in = [sem(f"w2_in{e}") for e in range(E)]
        out_done = sem("out_done")
        zeros_set = sem("zeros_set")
        consts_cast = sem("consts_cast")
        a_exp = sem("a_exp")
        a_neg_done = sem("a_neg_done")
        w_hi_done = sem("w_hi_done")
        w_lo_done = sem("w_lo_done")
        norm_stats = sem("norm_stats")
        norm_rstd = sem("norm_rstd")
        norm_done = sem("norm_done")
        scratch_ready = sem("scratch_ready")
        scratch_read = sem("scratch_read")
        x_hi_done = sem("x_hi_done")
        gate_step = sem("gate_step")
        gate_exp = sem("gate_exp")
        gate_done = sem("gate_done")
        up_b_done = sem("up_b_done")
        up_done = sem("up_done")
        act_done = sem("act_done")
        b_copied = sem("b_copied")
        q_done = sem("q_done")
        h_dve_done = sem("h_dve_done")
        h_pool_done = sem("h_pool_done")
        down_done = sem("down_done")
        scaled_done = sem("scaled_done")
        added = sem("added")
        conv_begun = sem("conv_begun")
        y_begun = sem("y_begun")
        conv_done = sem("conv_done")
        tanh_u_done = sem("tanh_u_done")
        u_done = sem("u_done")
        tanh_z = sem("tanh_z")
        dt_low_done = sem("dt_low_done")
        bc_hi_done = sem("bc_hi_done")
        bc_done = sem("bc_done")
        sp_exp_done = sem("sp_exp_done")
        sp_one_done = sem("sp_one_done")
        sp_ln_done = sem("sp_ln_done")
        sp_steps = sem("sp_steps")
        dt_done = sem("dt_done")
        mamba_set = sem("mamba_set")
        decay_done = sem("decay_done")
        B_done = sem("B_done")
        drive_done = sem("drive_done")
        scan_done = sem("scan_done")
        C_done = sem("C_done")
        prod_done = sem("prod_done")
        y_added = sem("y_added")
        gated = sem("gated")
        dve_chain = sem("dve_chain")
        pool_chain = sem("pool_chain")

        EARLY, LATE = 4, 6
        block = ctx.enter_context(nc.Block())

        def rows(name, b):
            return res[:, b * TILES:(b + 1) * TILES, :]

        def tile(ap, j):
            return ap[:, j * 128:(j + 1) * 128]

        def pool_chunks(n):
            return sum(1 for g in range(n % FC) if g in POOL_CHUNKS) + n // FC * len(POOL_CHUNKS)

        def h_is_done(engine, g):
            if g % FC in POOL_CHUNKS:
                engine.wait_ge(h_pool_done, pool_chunks(g + 1))
            else:
                engine.wait_ge(h_dve_done, g + 1 - pool_chunks(g + 1))

        @block.sync
        def _(sp):
            xv = x.rearrange("(t p) h -> p t h", p=128)
            ov = out.rearrange("(t p) h -> p t h", p=128)

            def load_w13(e):
                if e >= RING_A:
                    sp.wait_ge(w_lo_done, e - RING_A + 1)
                sp.dma_start(staged[:, e % RING_A, :], w13[:, e, :]).then_inc(w13_in[e % RING_A], 16)

            sp.dma_start(rows(res, 0), xv[:, 0:TILES, :]).then_inc(x_in[0], 16)
            load_w13(0)
            sp.dma_start(eye[:, :], ident).then_inc(consts_in, 16)
            sp.dma_start(gate_sb[:, :], gate).then_inc(consts_in, 16)
            sp.dma_start(pick_sb[:, :], pick).then_inc(consts_in, 16)
            sp.dma_start(rank_sb[:, :], rank).then_inc(consts_in, 16)
            load_w13(1)
            sp.dma_start(w2_sb[:, 0], w2[:, 0]).then_inc(w2_in[0], 16)
            load_w13(2)
            load_w13(3)
            for b in range(1, B):
                sp.dma_start(rows(res, b), xv[:, b * TILES:(b + 1) * TILES, :]).then_inc(x_in[b], 16)
            for dst, src in ((vec, vecs), (a_neg, a_log), (in_w, in_proj), (x_w, x_proj), (dt_w, dt_proj),
                             (out_w, out_proj)):
                at = (slice(None),) * len(dst.shape)
                sp.dma_start(dst[at], src).then_inc(late_in, 16)
            for e in range(1, E):
                sp.dma_start(w2_sb[:, e], w2[:, e]).then_inc(w2_in[e], 16)
                if e + 3 < E:
                    load_w13(e + 3)
            for b in range(B):
                sp.wait_ge(scratch_read, USE["post", 2, b] + 1)
                sp.dma_start(ov[:, b * TILES:(b + 1) * TILES, :], rows(res, b)).then_inc(out_done, 16)
            sp.wait_ge(out_done, 16 * B)

        @block.gpsimd
        def _(pool):
            nc.gpsimd.memset(h[:, 0, :], 0.0).then_inc(zeros_set, 1)
            nc.gpsimd.memset(mhalf[:, :], -0.5).then_inc(pool_chain, 1)
            pool.wait_ge(pool_chain, 1)
            chain = [1]

            def stats_(kind, b):
                n = NORM["norm", kind, b]
                pool.wait_ge(norm_stats, n + 1)
                nc.gpsimd.tensor_scalar(rstd[:, n % 2, :], mv[:, n % 2, :, 1], LN_EPS, None, ALU.add).then_inc(pool_chain, 1)
                chain[0] += 1
                pool.wait_ge(pool_chain, chain[0])
                nc.gpsimd.tensor_tensor(rstd[:, n % 2, :], rstd[:, n % 2, :], mhalf[:, :], ALU.pow).then_inc(norm_rstd, 1)

            def up(k, f):
                if f not in POOL_CHUNKS:
                    return
                g = k * FC + f
                pool.wait_ge(b_copied, pool_chunks(g + 1))
                pool.wait_ge(q_done, g + 1)
                nc.gpsimd.tensor_tensor(h[:, g % RING_H, :], h[:, g % RING_H, :], act[:, g % RING_Q, :],
                                        ALU.mult).then_inc(h_pool_done, 1)

            def down(k, f):
                ffn, b, e = JOBS[k]
                if f < FC - 1 or e == 0:
                    return
                n = ADDS[k]
                pool.wait_ge(scaled_done, k + 1)
                if n > 1:
                    pool.wait_ge(added, n - 1)
                nc.gpsimd.tensor_tensor(ysum[:, ffn - 1, :], ysum[:, ffn - 1, :], scaled[:, n % 2, :],
                                        ALU.add).then_inc(added, 1)

            def read(b, s):
                n = b * DS + s
                pool.wait_ge(prod_done, n + 1)
                if n:
                    pool.wait_ge(y_added, n)
                if s == 0:
                    pool.wait_ge(y_begun, DH * (b + 1))
                nc.gpsimd.tensor_tensor(y[:, :, :], y[:, :, :], prod[:, n % 2], ALU.add).then_inc(y_added, 1)

            def mamba_set_(b):
                pool.wait_ge(dt_done, b + 1)
                if b:
                    pool.wait_ge(drive_done, DS * b)
                for i in range(DH):
                    nc.gpsimd.tensor_tensor(dtu[:, i, :], dt[:, i, :], u[:, i, :], ALU.mult).then_inc(mamba_set, 1)

            stages = {"stats": stats_, "up": up, "down": down, "read": read, "mamba_set": mamba_set_}
            for stage, *which in STEPS:
                if stage in stages:
                    stages[stage](*which)

        @block.scalar
        def _(sc):
            sc.wait_ge(pool_chain, 1)
            nc.scalar.activation(first[:, :], mhalf[:, :], ACT.Exp)

            def split(e):
                sc.wait_ge(w13_in[e % RING_A], 16 * (e // RING_A + 1))
                nc.scalar.activation(w13_hi[:, e, :], staged[:, e % RING_A, :], ACT.Copy).then_inc(w_hi_done, 1)
                if e == RING_A:
                    sc.wait_ge(late_in, 16 * LATE)
                    nc.scalar.activation(a_neg[:, :, :], a_neg[:, :, :], ACT.Exp).then_inc(a_exp, 1)

            def turn(kind, b):
                n = USE["turn", kind, b]
                sc.wait_ge(scratch_ready, n + 1)
                if kind == "mid":
                    nc.scalar.activation(xm[:, :], scratch[:, :], ACT.Copy).then_inc(scratch_read, 1)
                else:
                    nc.scalar.activation(x_hi[:, b, :], scratch[:, :], ACT.Copy).then_inc(x_hi_done, 1)

            def gate(kind, b):
                sc.wait_ge(scratch_ready, USE["gate", kind, b] + 1)
                nc.scalar.activation(logits, scratch[0:E, :], ACT.Copy).then_inc(scratch_read, 1)

            def gate_exp_(kind, b):
                n = GATE["gate", kind, b]
                sc.wait_ge(gate_step, (n + 1) * CHOOSE_PARTS + n * (WEIGH_PARTS - 1))
                nc.scalar.activation(expo[:, :, :, :], gap[:, :, :, :], ACT.Exp, scale=-1.0).then_inc(gate_exp, 1)

            def gate_turn(kind, b):
                sc.wait_ge(scratch_ready, USE["gate_turn", kind, b] + 1)
                nc.scalar.activation(wt[:, b, :], scratch_bf[0:3 * E, 0:L], ACT.Copy).then_inc(scratch_read, 1)

            def up(k, f):
                g = k * FC + f
                if f in POOL_CHUNKS:
                    sc.wait_ge(up_b_done, g + 1)
                    if g >= RING_H:
                        sc.wait_ge(down_done, g - RING_H + 1)
                    nc.scalar.activation(h[:, g % RING_H, :], ps_b[g % 2][:, :], ACT.Copy).then_inc(b_copied, 1)
                sc.wait_ge(up_done, g + 1)
                if g >= RING_Q:
                    h_is_done(sc, g - RING_Q)
                nc.scalar.activation(act[:, g % RING_Q, :], ps_a[g % 2][:, :], ACT.Tanh, scale=0.5).then_inc(act_done, 1)

            def spread_(k):
                sc.wait_ge(scratch_ready, USE["spread", k] + 1)
                if k >= 2:
                    sc.wait_ge(scaled_done, k - 1)
                nc.scalar.activation(spread[:, k % 2, :], scratch[:, :], ACT.Copy).then_inc(scratch_read, 1)

            def in_proj_(b, i):
                sc.wait_ge(scratch_ready, USE["in_proj", b, i] + 1)
                if i < DH:
                    if b:
                        sc.wait_ge(bc_done, b)
                        sc.wait_ge(scratch_read, USE["dt_proj", b - 1, DH - 1] + 1)
                    nc.scalar.activation(xs[:, i, DC - 1:], scratch[:, :], ACT.Copy).then_inc(scratch_read, 1)
                else:
                    if b:
                        sc.wait_ge(gated, b)
                    nc.scalar.activation(silu_z[:, i - DH, :], scratch[:, :], ACT.Tanh, scale=0.5).then_inc(tanh_z, 1)

            def conv_(b, i, c):
                if c:
                    return
                if b:
                    sc.wait_ge(mamba_set, DH * b)
                    sc.wait_ge(y_begun, DH * b)
                sc.wait_ge(scratch_read, USE["in_proj", b, i] + 1)
                nc.scalar.activation(u[:, i, :], xs[:, i, 0:L], ACT.Identity, bias=vec[:, i, DC:DC + 1],
                                     scale=vec[:, i, 0:1]).then_inc(conv_begun, 1)

            def y_begin(b):
                sc.wait_ge(u_done, DH * (b + 1))
                if b:
                    sc.wait_ge(gated, b)
                for i in range(DH):
                    nc.scalar.activation(y[:, i, :], u[:, i, :], ACT.Copy, scale=vec[:, i, DC + 2:DC + 3]).then_inc(y_begun, 1)

            def tanh_u_(b, i):
                sc.wait_ge(conv_done, (DC - 1) * (DH * b + i + 1))
                nc.scalar.activation(tanh_u[:, i, :], u[:, i, :], ACT.Tanh, scale=0.5).then_inc(tanh_u_done, 1)

            def x_dbl(b):
                sc.wait_ge(scratch_ready, USE["x_dbl", b] + 1)
                nc.scalar.activation(dt_low[:, :], scratch[BC_ROWS:BC_ROWS + DR, :], ACT.Copy, scale=0.5).then_inc(dt_low_done, 1)
                if b >= 2:
                    sc.wait_ge(B_done, DS * (b - 1))
                    sc.wait_ge(C_done, DS * (b - 1))
                nc.scalar.activation(bc[:, b % 2, :], scratch[0:BC_ROWS, :], ACT.Copy, scale=0.5).then_inc(bc_hi_done, 1)

            def dt_proj_(b, i):
                sc.wait_ge(scratch_ready, USE["dt_proj", b, i] + 1)
                bias = vec[:, i, DC + 1:DC + 2]
                if b:
                    sc.wait_ge(scan_done, DH * DS * b)
                    sc.wait_ge(prod_done, DS * b)
                nc.scalar.activation(dt_relu[:, i, :], scratch[:, :], ACT.Relu, bias=bias)
                nc.scalar.activation(sp_exp[:, i, :], scratch[:, :], ACT.Abs, bias=bias).then_inc(scratch_read, 1)

            def sp_exp_(b):
                sc.wait_ge(scratch_read, USE["dt_proj", b, DH - 1] + 1)
                nc.scalar.activation(sp_exp[:, :, :], sp_exp[:, :, :], ACT.Exp, scale=-1.0).then_inc(sp_exp_done, 1)

            def sp_ln_(b):
                sc.wait_ge(sp_one_done, b + 1)
                nc.scalar.activation(sp_ln, sp_one, ACT.Ln).then_inc(sp_ln_done, 1)

            def decays(b, w):
                sc.wait_ge(dt_done, b + 1)
                if b == 0 and w == 0:
                    sc.wait_ge(w_lo_done, E)
                    sc.wait_ge(a_neg_done, 1)
                for s in (2 * w, 2 * w + 1):
                    n = b * DS + s
                    if n >= RING_A:
                        sc.wait_ge(scan_done, DH * (n - RING_A + 1))
                    for i in range(DH):
                        nc.scalar.activation(decay[:, n % RING_A, i * L:(i + 1) * L], dt[:, i, :], ACT.Exp,
                                             scale=a_neg[:, i, s:s + 1]).then_inc(decay_done, 1)

            stages = {"split": split, "turn": turn, "gate": gate, "gate_exp": gate_exp_, "gate_turn": gate_turn, "up": up,
                      "spread": spread_, "in_proj": in_proj_, "conv": conv_, "y_begin": y_begin, "tanh_u": tanh_u_, "x_dbl": x_dbl,
                      "dt_proj": dt_proj_, "sp_exp": sp_exp_, "sp_ln": sp_ln_, "decays": decays}
            for stage, *which in STEPS:
                if stage in stages:
                    stages[stage](*which)

        @block.tensor
        def _(pe):
            zeros = h[:, 0, :].bitcast(bf16)[:, 0:L]
            pe.wait_ge(zeros_set, 1)
            for _ in range(WARMING):
                nc.tensor.matmul(ps_a[1][:, :], zeros[:, 0:128], zeros, start=True, stop=True)
            pe.wait_ge(consts_in, 16 * EARLY)
            pe.wait_ge(consts_cast, 1)

            def begin(*step):
                n = USE[step]
                if n:
                    pe.wait_ge(scratch_read, n)
                return n

            def turn(kind, b):
                begin("turn", kind, b)
                pe.wait_ge(norm_done, NORM["norm", kind, b] + 1)
                rows_ = xm[:, :].rearrange("p (t h) -> p t h", h=H) if kind == "mid" else normed
                for j in range(TILES):
                    last = nc.tensor.transpose(tile(scratch, j), rows_[:, j, :], eye[:, :])
                last.then_inc(scratch_ready, 1)

            def gate_(kind, b):
                begin("gate", kind, b)
                for n, (gg, xx) in enumerate(((gate_hi, x_hi), (gate_hi, x_lo), (gate_lo, x_hi))):
                    last = nc.tensor.matmul(scratch[0:E, :], gg[:, :], xx[:, b, :], start=(n == 0), stop=(n == 2))
                last.then_inc(scratch_ready, 1)

            def gate_rows(kind, b):
                begin("gate_rows", kind, b)
                for j in range(TILES):
                    last = nc.tensor.transpose(scratch[:, j * E:(j + 1) * E], tile(logits, j), eye[0:E, 0:E])
                last.then_inc(scratch_ready, 1)

            def gate_turn(kind, b):
                begin("gate_turn", kind, b)
                pe.wait_ge(gate_done, GATE["gate", kind, b] + 1)
                for j in range(TILES):
                    last = nc.tensor.transpose(tile(scratch_bf[0:3 * E, :], j),
                                               wparts[:, j, :, :].rearrange("p c e -> p (c e)"), eye_bf[:, :])
                last.then_inc(scratch_ready, 1)

            def products(bank_, at, e, b):
                hi, lo = w13_hi[:, e, at:at + 128], w13_lo[:, e, at:at + 128]
                nc.tensor.matmul(bank_[:, :], hi, x_hi[:, b, :], start=True, stop=False)
                nc.tensor.matmul(bank_[:, :], hi, x_lo[:, b, :], start=False, stop=False)
                return nc.tensor.matmul(bank_[:, :], lo, x_hi[:, b, :], start=False, stop=True)

            def up(k, f):
                ffn, b, e = JOBS[k]
                g = k * FC + f
                if (ffn, b) == (1, 0) and f == 0:
                    pe.wait_ge(w_lo_done, e + 1)
                if e == 0 and f == 0:
                    pe.wait_ge(scratch_read, USE["turn", "in" if ffn == 1 else "out", b] + 1)
                if g >= 2:
                    if f in POOL_CHUNKS:
                        pe.wait_ge(b_copied, pool_chunks(g - 1))
                    else:
                        h_is_done(pe, g - 2)
                products(ps_b[g % 2], F + f * 128, e, b).then_inc(up_b_done, 1)
                if g >= 2:
                    pe.wait_ge(q_done, g - 1)
                products(ps_a[g % 2], f * 128, e, b).then_inc(up_done, 1)

            def spread_(k):
                ffn, b, e = JOBS[k]
                begin("spread", k)
                nc.tensor.matmul(scratch[:, :], pick_bf[0:3 * E, 32 + e:33 + e].broadcast_to([3 * E, 128]),
                                 wt[:, b, :], start=True, stop=True).then_inc(scratch_ready, 1)

            def down(k, f):
                ffn, b, e = JOBS[k]
                g = k * FC + f
                if f == 0:
                    if (ffn, b) == (1, 0):
                        pe.wait_ge(w2_in[e], 16)
                    if k:
                        pe.wait_ge(scaled_done, k)
                h_is_done(pe, g)
                nc.tensor.matmul(ps_down[:, :], w2_sb[:, e, f, :], h[:, g % RING_H, :],
                                 start=(f == 0), stop=(f == FC - 1)).then_inc(down_done, 1)

            def post(ffn, b):
                begin("post", ffn, b)
                pe.wait_ge(added, ADDS[LAST_JOB[ffn, b]])
                for j in range(TILES):
                    last = nc.tensor.transpose(tile(scratch, j), tile(ysum[:, ffn - 1, :], j), eye[:, :])
                last.then_inc(scratch_ready, 1)

            def in_proj_(b, i):
                begin("in_proj", b, i)
                if b == 0 and i == 0:
                    pe.wait_ge(late_in, 16 * LATE)
                nc.tensor.matmul(scratch[:, :], tile(in_w, i), xm[:, :], start=True, stop=True).then_inc(scratch_ready, 1)

            def x_dbl(b):
                begin("x_dbl", b)
                pe.wait_ge(u_done, DH * (b + 1))
                for i in range(DH):
                    last = nc.tensor.matmul(scratch[0:BC_ROWS + DR, :], x_w[:, i, :], u[:, i, :],
                                            start=(i == 0), stop=(i == DH - 1))
                last.then_inc(scratch_ready, 1)

            def dt_proj_(b, i):
                begin("dt_proj", b, i)
                pe.wait_ge(dt_low_done, b + 1)
                nc.tensor.matmul(scratch[:, :], tile(dt_w, i), dt_low[:, :], start=True, stop=True)\
                    .then_inc(scratch_ready, 1)

            def spread_B(b, s):
                n = b * DS + s
                pe.wait_ge(bc_done, b + 1)
                if n:
                    pe.wait_ge(drive_done, n)
                nc.tensor.matmul(ps_B[:, :], pick_bf[0:BC_ROWS, s:s + 1].broadcast_to([BC_ROWS, 128]), bc[:, b % 2, :],
                                 start=True, stop=True).then_inc(B_done, 1)

            def spread_C(b, s):
                n = b * DS + s
                if n:
                    pe.wait_ge(prod_done, n)
                nc.tensor.matmul(ps_C[:, :], pick_bf[0:BC_ROWS, DS + s:DS + s + 1].broadcast_to([BC_ROWS, 128]),
                                 bc[:, b % 2, :], start=True, stop=True).then_inc(C_done, 1)

            def out_proj_(b):
                begin("out_proj", b)
                pe.wait_ge(gated, b + 1)
                for j in range(TILES):
                    for i in range(DH):
                        last = nc.tensor.matmul(tile(scratch, j), tile(y[:, i, :], j), out_w[:, i, :],
                                                start=(i == 0), stop=(i == DH - 1))
                last.then_inc(scratch_ready, 1)

            stages = {"turn": turn, "gate": gate_, "gate_rows": gate_rows, "gate_turn": gate_turn, "up": up, "spread": spread_,
                      "down": down, "post": post, "in_proj": in_proj_, "x_dbl": x_dbl, "dt_proj": dt_proj_,
                      "B": spread_B, "C": spread_C, "out_proj": out_proj_}
            for stage, *which in STEPS:
                if stage in stages:
                    stages[stage](*which)

        @block.vector
        def _(dve):
            chain = [0]

            def then(instruction):
                chain[0] += 1
                instruction.then_inc(dve_chain, 1)
                dve.wait_ge(dve_chain, chain[0])

            TT, TS, STT = nc.vector.tensor_tensor, nc.vector.tensor_scalar, nc.vector.scalar_tensor_tensor

            nc.vector.memset(xs[:, :, 0:DC - 1], 0.0)
            def cast_consts():
                dve.wait_ge(consts_in, 16 * EARLY)
                nc.vector.tensor_copy(eye_bf[:, :], eye[:, :])
                nc.vector.tensor_copy(pick_bf[:, :], pick_sb[:, :])
                then(nc.vector.tensor_copy(gate_hi[:, :], gate_sb[:, :]))
                TT(gate_lo[:, :], gate_sb[:, :], gate_hi[:, :].bitcast(fp32), ALU.subtract).then_inc(consts_cast, 1)

            def split(e):
                dve.wait_ge(w_hi_done, e + 1)
                TT(w13_lo[:, e, :], staged[:, e % RING_A, :], w13_hi[:, e, :].bitcast(fp32),
                   ALU.subtract).then_inc(w_lo_done, 1)
                if e == RING_A:
                    dve.wait_ge(a_exp, 1)
                    TS(a_neg[:, :, :], a_neg[:, :, :], -1.0, None, ALU.mult).then_inc(a_neg_done, 1)

            def stats_(kind, b):
                n = NORM["norm", kind, b]
                xx = rows(res, b)
                if n:
                    dve.wait_ge(norm_stats, n)
                if n >= 2:
                    dve.wait_ge(norm_done, n - 1)
                if kind == "in":
                    dve.wait_ge(x_in[b], 16)
                else:
                    dve.wait_ge(scratch_read, USE[("post", 1, b) if kind == "mid" else ("out_proj", b)] + 1)
                for j in range(TILES):
                    last = nc.vector.bn_stats(stats[:, j, :], xx[:, j, :])
                then(last)
                for j in range(TILES):
                    last = nc.vector.bn_aggr(mv[:, n % 2, j, :], stats[:, j, :])
                last.then_inc(norm_stats, 1)

            def norm(kind, b):
                n = NORM["norm", kind, b]
                xx = rows(res, b)
                dve.wait_ge(norm_rstd, n + 1)
                if kind == "mid":
                    dst = xm[:, :].rearrange("p (t h) -> p t h", h=H)
                    if b:
                        dve.wait_ge(scratch_ready, USE["in_proj", b - 1, 2 * DH - 1] + 1)
                else:
                    dst = normed
                    others = [s[1:] for s in STEPS if s[0] == "norm" and s[1] != "mid"]
                    at = others.index((kind, b))
                    if at:
                        dve.wait_ge(scratch_ready, USE[("gate_rows",) + tuple(others[at - 1])] + 1)
                for j in range(TILES):
                    last = TS(dst[:, j, :], xx[:, j, :], mv[:, n % 2, j, 0:1], rstd[:, n % 2, j:j + 1], ALU.subtract, ALU.mult)
                last.then_inc(norm_done, 1)

            def read_turn(kind, b):
                dve.wait_ge(x_hi_done, HALVED["turn", kind, b] + 1)
                TT(x_lo[:, b, :], scratch[:, :], x_hi[:, b, :].bitcast(fp32), ALU.subtract).then_inc(scratch_read, 1)

            gate_steps = [0]

            def each(ap):
                return ap.unsqueeze(2).broadcast_to([128, TILES, E])

            def counted(instruction):
                gate_steps[0] += 1
                instruction.then_inc(gate_step, 1)

            def read_gate_rows(kind, b):
                dve.wait_ge(scratch_ready, USE["gate_rows", kind, b] + 1)
                nc.vector.tensor_copy(score[:, :, :].rearrange("p t e -> p (t e)"), scratch[:, 0:TILES * E])\
                    .then_inc(scratch_read, 1)

            def choose(kind, b, part):
                if part == 0:
                    dve.wait_ge(scratch_read, USE["gate_rows", kind, b] + 1)
                else:
                    dve.wait_ge(gate_step, gate_steps[0])
                size = keep[:, 1]
                if part == 0:
                    STT(size, score[:, :, :], -1.0, score[:, :, :], ALU.mult, ALU.max)
                    counted(nc.vector.tensor_reduce(top[:, 0], score[:, :, :], AX.X, ALU.max))
                elif part == 1:
                    TT(gap[:, 0], each(top[:, 0]), score[:, :, :], ALU.subtract)
                    counted(TT(hot[:, 0], score[:, :, :], each(top[:, 0]), ALU.is_equal))
                elif part in (2, 8):
                    i = part // 8
                    if i == 0:
                        TT(keep[:, 0], size, each(top[:, 0]), ALU.max)
                    else:
                        TT(size, size, each(top[:, 1]), ALU.max)
                    counted(TT(hot[:, i], hot[:, i], rank_sb[:, :].unsqueeze(1).broadcast_to([128, TILES, E]), ALU.mult))
                elif part in (3, 9):
                    counted(nc.vector.tensor_reduce(first[:, :], hot[:, part // 8], AX.X, ALU.max))
                elif part in (4, 10):
                    counted(TT(hot[:, part // 8], hot[:, part // 8], each(first[:, :]), ALU.is_equal))
                elif part == 5:
                    counted(STT(gtmp[:, :, :], hot[:, 0], -3.0e38, score[:, :, :], ALU.mult, ALU.add))
                elif part == 6:
                    counted(nc.vector.tensor_reduce(top[:, 1], gtmp[:, :, :], AX.X, ALU.max))
                elif part == 7:
                    TT(gap[:, 1], each(top[:, 1]), score[:, :, :], ALU.subtract)
                    counted(TT(hot[:, 1], gtmp[:, :, :], each(top[:, 1]), ALU.is_equal))
                elif part == 11:
                    counted(STT(keep[:, :, :, :], keep[:, :, :, :], JITTER, gap[:, :, :, :], ALU.mult, ALU.is_ge))
                elif part == 12:
                    TT(keep[:, 1], keep[:, 1], hot[:, 0], ALU.subtract)
                    counted(TS(gap[:, :, :, :], gap[:, :, :, :], 0.0, None, ALU.max))

            def weigh(kind, b, part):
                if part == 0:
                    dve.wait_ge(gate_exp, GATE["gate", kind, b] + 1)
                else:
                    dve.wait_ge(gate_step, gate_steps[0])
                w = expo[:, 0]
                if part == 0:
                    counted(TT(expo[:, :, :, :], expo[:, :, :, :], keep[:, :, :, :], ALU.mult))
                elif part == 1:
                    counted(nc.vector.tensor_reduce(total[:, :, :], expo[:, :, :, :], AX.X, ALU.add))
                elif part == 2:
                    counted(nc.vector.reciprocal(total[:, :, :], total[:, :, :]))
                elif part == 3:
                    TT(hot[:, 0], hot[:, 0], each(total[:, 0]), ALU.mult)
                    counted(TT(hot[:, 1], hot[:, 1], each(total[:, 1]), ALU.mult))
                elif part == 4:
                    counted(TT(w, hot[:, 0], hot[:, 1], ALU.add))
                elif part == 5:
                    if GATE["gate", kind, b]:
                        former = [s for s in STEPS if s[0] == "gate_turn"]
                        former = former[former.index(("gate_turn", kind, b)) - 1]
                        dve.wait_ge(scratch_ready, USE[former] + 1)
                    counted(nc.vector.tensor_copy(wparts[:, :, 0, :], w))
                elif part == 6:
                    counted(TT(gtmp[:, :, :], w, wparts[:, :, 0, :], ALU.subtract))
                elif part == 7:
                    counted(nc.vector.tensor_copy(wparts[:, :, 1, :], gtmp[:, :, :]))
                elif part == 8:
                    TT(wparts[:, :, 2, :], gtmp[:, :, :], wparts[:, :, 1, :], ALU.subtract).then_inc(gate_done, 1)

            def up(k, f):
                g = k * FC + f
                dve.wait_ge(act_done, g + 1)
                STT(act[:, g % RING_Q, :], act[:, g % RING_Q, :], 1.0, ps_a[g % 2][:, :], ALU.add, ALU.mult).then_inc(q_done, 1)
                if f in POOL_CHUNKS:
                    return
                if g >= RING_H:
                    dve.wait_ge(down_done, g - RING_H + 1)
                dve.wait_ge(q_done, g + 1)
                TT(h[:, g % RING_H, :], act[:, g % RING_Q, :], ps_b[g % 2][:, :], ALU.mult).then_inc(h_dve_done, 1)

            def down(k, f):
                ffn, b, e = JOBS[k]
                if f < FC - 1:
                    return
                dve.wait_ge(down_done, (k + 1) * FC)
                dve.wait_ge(scratch_read, USE["spread", k] + 1)
                if e == 0:
                    dst = ysum[:, ffn - 1, :]
                    if b:
                        dve.wait_ge(scratch_ready, USE["post", ffn, b - 1] + 1)
                else:
                    n = ADDS[k]
                    dst = scaled[:, n % 2, :]
                    if n > 2:
                        dve.wait_ge(added, n - 2)
                TT(dst, ps_down[:, :], spread[:, k % 2, :], ALU.mult).then_inc(scaled_done, 1)

            def read_post(ffn, b):
                dve.wait_ge(scratch_ready, USE["post", ffn, b] + 1)
                xx = rows(res, b).rearrange("p t h -> p (t h)")
                STT(xx, scratch[:, :], 0.25, xx, ALU.mult, ALU.add).then_inc(scratch_read, 1)

            def conv_(b, i, c):
                if c == 0:
                    return
                if c == 1:
                    dve.wait_ge(conv_begun, DH * b + i + 1)
                else:
                    dve.wait_ge(conv_done, (DC - 1) * (b * DH + i) + c - 1)
                STT(u[:, i, :], xs[:, i, c:c + L], vec[:, i, c:c + 1], u[:, i, :], ALU.mult, ALU.add).then_inc(conv_done, 1)

            def conv_silu(b, i):
                dve.wait_ge(tanh_u_done, DH * b + i + 1)
                STT(u[:, i, :], tanh_u[:, i, :], 1.0, u[:, i, :], ALU.add, ALU.mult).then_inc(u_done, 1)

            def read_in_proj(b, i):
                if i >= DH:
                    dve.wait_ge(tanh_z, DH * b + i - DH + 1)
                    STT(silu_z[:, i - DH, :], silu_z[:, i - DH, :], 1.0, scratch[:, :], ALU.add,
                        ALU.mult).then_inc(scratch_read, 1)

            def read_x_dbl(b):
                dve.wait_ge(bc_hi_done, b + 1)
                STT(bc_rest[:, :], scratch[0:BC_ROWS, :], 0.5, bc[:, b % 2, :], ALU.mult, ALU.subtract)\
                    .then_inc(scratch_read, 1)
                dve.wait_ge(scratch_read, USE["x_dbl", b] + 1)
                nc.vector.tensor_copy(bc[32:64, b % 2, :], bc_rest[32:64, :])
                then(nc.vector.tensor_copy(bc[64:96, b % 2, :], bc_rest[64:96, :]))
                TT(bc[64:96, b % 2, :], bc_rest[64:96, :], bc[64:96, b % 2, :], ALU.subtract).then_inc(bc_done, 1)

            def sp_one_(b):
                dve.wait_ge(sp_exp_done, b + 1)
                if b:
                    dve.wait_ge(y_added, DS * b)
                TS(sp_one, sp_exp[:, :, :], 1.0, None, ALU.add).then_inc(sp_one_done, 1)

            def sp_rest(b):
                dve.wait_ge(sp_one_done, b + 1)
                STT(sp_exp[:, :, :], sp_one, -1.0, sp_exp[:, :, :], ALU.add, ALU.subtract).then_inc(sp_steps, 1)

            def sp_mask(b):
                dve.wait_ge(sp_ln_done, b + 1)
                STT(sp_ln, sp_one, 1.0, sp_ln, ALU.is_gt, ALU.mult).then_inc(sp_steps, 1)

            def sp_diff(b):
                dve.wait_ge(sp_steps, 3 * b + 2)
                TT(sp_exp[:, :, :], sp_ln, sp_exp[:, :, :], ALU.subtract).then_inc(sp_steps, 1)

            def sp_dt(b):
                dve.wait_ge(sp_steps, 3 * b + 3)
                if b:
                    dve.wait_ge(decay_done, DH * DS * b)
                TT(dt[:, :, :], dt_relu[:, :, :], sp_exp[:, :, :], ALU.add).then_inc(dt_done, 1)

            def drive_(b, s):
                n = b * DS + s
                dve.wait_ge(B_done, n + 1)
                if s == 0:
                    dve.wait_ge(mamba_set, DH * (b + 1))
                else:
                    dve.wait_ge(scan_done, DH * n)
                TT(drive[:, :, :], dtu[:, :, :], ps_B[:, :].unsqueeze(1).broadcast_to([128, DH, L]),
                   ALU.mult).then_inc(drive_done, 1)

            def scan(b, s, i):
                n = b * DS + s
                dve.wait_ge(decay_done, DH * n + i + 1)
                dve.wait_ge(drive_done, n + 1)
                if n:
                    dve.wait_ge(prod_done, n)
                nc.vector.tensor_tensor_scan(state[:, i, :], decay[:, n % RING_A, i * L:(i + 1) * L], drive[:, i, :],
                                             0.0, ALU.mult, ALU.add).then_inc(scan_done, 1)

            def read(b, s):
                n = b * DS + s
                dve.wait_ge(C_done, n + 1)
                dve.wait_ge(scan_done, DH * (n + 1))
                if n >= 2:
                    dve.wait_ge(y_added, n - 1)
                TT(prod[:, n % 2], state[:, :, :], ps_C[:, :].unsqueeze(1).broadcast_to([128, DH, L]),
                   ALU.mult).then_inc(prod_done, 1)

            def gate_y(b):
                dve.wait_ge(y_added, DS * (b + 1))
                STT(y[:, :, :], y[:, :, :], 0.25, silu_z[:, :, :], ALU.mult, ALU.mult).then_inc(gated, 1)

            def read_out_proj(b):
                dve.wait_ge(scratch_ready, USE["out_proj", b] + 1)
                xx = rows(res, b).rearrange("p t h -> p (t h)")
                TT(xx, scratch[:, :], xx, ALU.add).then_inc(scratch_read, 1)

            stages = {"cast": cast_consts, "split": split, "stats": stats_, "norm": norm, "read_turn": read_turn, "read_gate_rows": read_gate_rows, "choose": choose,
                      "weigh": weigh, "up": up, "down": down, "read_post": read_post, "read_in_proj": read_in_proj,
                      "conv": conv_, "conv_silu": conv_silu, "read_x_dbl": read_x_dbl, "sp_one": sp_one_,
                      "sp_rest": sp_rest, "sp_mask": sp_mask, "sp_diff": sp_diff, "sp_dt": sp_dt, "drive": drive_, "scan": scan,
                      "read": read, "gate_y": gate_y, "read_out_proj": read_out_proj}
            for stage, *which in STEPS:
                if stage in stages:
                    stages[stage](*which)


def kernel(L0_attn_x, L0_attn_in_proj_w, L0_attn_conv_w, L0_attn_conv_b, L0_attn_x_proj_w, L0_attn_dt_proj_w,
           L0_attn_dt_proj_b, L0_attn_A_log, L0_attn_D, L0_attn_out_proj_w, L0_ffn_gate_w, L0_ffn_w1,
           L0_ffn_w2, L0_ffn_w3):
    import numpy as np
    import concourse.bacc as bacc
    from concourse.bass_utils import run_bass_kernel_spmd

    def halves(a):
        a = np.asarray(a)
        return a.reshape(DH, 128, -1).transpose(1, 0, 2)

    w1, w3, w2 = (np.asarray(a) for a in (L0_ffn_w1, L0_ffn_w3, L0_ffn_w2))
    xp = np.asarray(L0_attn_x_proj_w)
    pick = np.zeros((128, 40), np.float32)
    for r in range(BC_ROWS):
        pick[r, r % 32] = 1
    for r in range(3 * E):
        pick[r, 32 + r % E] = 1
    arrays = {
        "x": np.asarray(L0_attn_x).reshape(B * L, H),
        "w13": np.concatenate([w1.transpose(2, 0, 1), w3.transpose(2, 0, 1)], axis=2),
        "w2": w2.transpose(2, 0, 1).reshape(FC, 128, E, H).transpose(1, 2, 0, 3),
        "gate": np.asarray(L0_ffn_gate_w).T,
        "in_proj": np.asarray(L0_attn_in_proj_w).T,
        "vecs": np.concatenate([halves(np.asarray(L0_attn_conv_w)[:, 0, :]), halves(L0_attn_conv_b),
                                halves(L0_attn_dt_proj_b), halves(L0_attn_D)], axis=2),
        "a_log": halves(L0_attn_A_log),
        "x_proj": halves(np.concatenate([xp[DR:], xp[DR:], xp[DR:], xp[:DR]], axis=0).T),
        "dt_proj": np.asarray(L0_attn_dt_proj_w).T,
        "out_proj": halves(np.asarray(L0_attn_out_proj_w).T),
        "ident": np.eye(128, dtype=np.float32),
        "pick": pick,
        "rank": np.tile(np.arange(E, 0, -1, dtype=np.float32), (128, 1)),
    }
    arrays = {name: np.ascontiguousarray(a) for name, a in arrays.items()}
    nc = bacc.Bacc("TRN2", target_bir_lowering=False, num_devices=1)
    args = [nc.dram_tensor(name, a.shape, mybir.dt.from_np(a.dtype), kind="ExternalInput").ap()
            for name, a in arrays.items()]
    out = nc.dram_tensor("out", (B * L, H), mybir.dt.float32, kind="ExternalOutput").ap()
    macaron_kernel(nc, *args, out)
    r = run_bass_kernel_spmd(nc, [arrays], core_ids=[0])
    return r.results[0]["out"].reshape(B, L, H)
```
